# Optimizing a Trainium2 kernel written in Bass

```python
import numpy as np
import jax
import jax.numpy as jnp

def _softmax(x, axis=-1):
    return jax.nn.softmax(x, axis=axis)

def _gelu(x):
    return jax.nn.gelu(x, approximate=True)

def _silu(x):
    return jax.nn.silu(x)

def _sigmoid(x):
    return jax.nn.sigmoid(x)

def _layernorm(x, axis=-1, eps=1e-05):
    m = jnp.mean(x, axis=axis, keepdims=True)
    v = jnp.var(x, axis=axis, keepdims=True)
    return (x - m) / jnp.sqrt(v + eps)

def _scatter_add(tgt, idx, src, axis=0):
    return tgt.at[idx].add(src)

def _segment_sum(src, seg, n):
    return jax.ops.segment_sum(src, seg, n)
kernel_name = 'mk_gnn_resnorm_d2_gnn_r32_3faa76'

def setup_inputs(seed: int=0):
    np.random.seed(seed)
    _w = jnp.asarray

    def _rec_inputs():
        import jax
        import jax.numpy as jnp
        _gk = jax.random.key(seed)
        x = -0.0001006 + 1 * jax.random.normal(jax.random.fold_in(_gk, 1), (3125, 96), jnp.float32)
        _s = jax.random.randint(jax.random.fold_in(_gk, 2), (50000,), 0, 3125, jnp.int32)
        _d = jax.random.randint(jax.random.fold_in(_gk, 3), (50000,), 0, 3125, jnp.int32)
        _loop = jnp.arange(3125, dtype=jnp.int32)
        src = jnp.concatenate([_s, _d, _loop])
        dst = jnp.concatenate([_d, _s, _loop])
        _o = jnp.argsort(dst, stable=True)
        src = src[_o]
        dst = dst[_o]
        edge_attr_17 = jax.random.uniform(jax.random.fold_in(_gk, 12), (103125, 17), jnp.float32, 0.0, 1)
        return (x, src, dst, edge_attr_17)
    x, src, dst, edge_attr_17 = _rec_inputs()

    def _L0_gnn_setup():
        import jax, jax.numpy as jnp
        import numpy as np
        N_NODES = 50000
        N_EDGES = 25000
        D_IN = 96
        D_OUT = 96
        key = jax.random.key(seed)
        k1, k2, k3, k4 = jax.random.split(key, 4)
        feat = jax.random.normal(k1, (N_NODES, D_IN), dtype=jnp.float32)
        std = (2.0 / (D_IN + D_OUT)) ** 0.5
        weight = jax.random.normal(k2, (D_IN, D_OUT), dtype=jnp.float32) * std
        bias = jnp.zeros((D_OUT,), dtype=jnp.float32)
        src = jax.random.randint(k3, (N_EDGES,), 0, N_NODES, dtype=jnp.int64)
        dst = jax.random.randint(k4, (N_EDGES,), 0, N_NODES, dtype=jnp.int64)
        return {'feat': feat, 'weight': weight, 'bias': bias, 'src': src, 'dst': dst}
    _L0_gnn_all = _L0_gnn_setup()
    _L0_gnn_in = {k: v for k, v in _L0_gnn_all.items() if k in ('weight', 'bias')}
    del _L0_gnn_all

    def _L1_gnn_setup():
        import jax, jax.numpy as jnp
        import numpy as np
        N = 50000
        E = 25000
        D = 96
        ED = 17
        key = jax.random.key(seed)
        ks = jax.random.split(key, 12)
        x = jax.random.normal(ks[0], (N, D), dtype=jnp.float32)
        edge_index = jax.random.randint(ks[1], (2, E), 0, N, dtype=jnp.int64)
        edge_attr = jax.random.uniform(ks[2], (E, ED), dtype=jnp.float32)
        s = 1.0 / np.sqrt(ED)
        W1 = jax.random.uniform(ks[3], (D, ED), jnp.float32, -s, s)
        b1 = jax.random.uniform(ks[4], (D,), jnp.float32, -s, s)
        s = 1.0 / np.sqrt(D)
        W2 = jax.random.uniform(ks[5], (D, D), jnp.float32, -s, s)
        b2 = jax.random.uniform(ks[6], (D,), jnp.float32, -s, s)
        Ws = jax.random.uniform(ks[7], (D, D), jnp.float32, -s, s)
        bs = jax.random.uniform(ks[8], (D,), jnp.float32, -s, s)
        Wn = jax.random.uniform(ks[9], (D, D), jnp.float32, -s, s)
        bn = jax.random.uniform(ks[10], (D,), jnp.float32, -s, s)
        return {'x': x, 'edge_index': edge_index, 'edge_attr': edge_attr, 'W1': W1, 'b1': b1, 'W2': W2, 'b2': b2, 'Ws': Ws, 'bs': bs, 'Wn': Wn, 'bn': bn}
    _L1_gnn_all = _L1_gnn_setup()
    _L1_gnn_in = {k: v for k, v in _L1_gnn_all.items() if k in ('W1', 'b1', 'W2', 'b2', 'Ws', 'bs', 'Wn', 'bn')}
    del _L1_gnn_all
    return {'x': x, 'src': src, 'dst': dst, 'edge_attr_17': edge_attr_17, 'L0_gnn_weight': _L0_gnn_in['weight'], 'L0_gnn_bias': _L0_gnn_in['bias'], 'L1_gnn_W1': _L1_gnn_in['W1'], 'L1_gnn_b1': _L1_gnn_in['b1'], 'L1_gnn_W2': _L1_gnn_in['W2'], 'L1_gnn_b2': _L1_gnn_in['b2'], 'L1_gnn_Ws': _L1_gnn_in['Ws'], 'L1_gnn_bs': _L1_gnn_in['bs'], 'L1_gnn_Wn': _L1_gnn_in['Wn'], 'L1_gnn_bn': _L1_gnn_in['bn']}

def reference(x, src, dst, edge_attr_17, L0_gnn_weight, L0_gnn_bias, L1_gnn_W1, L1_gnn_b1, L1_gnn_W2, L1_gnn_b2, L1_gnn_Ws, L1_gnn_bs, L1_gnn_Wn, L1_gnn_bn):
    import jax
    import jax.numpy as jnp

    def _L0_gnn_ref(feat, weight, bias, src, dst):
        import jax, jax.numpy as jnp
        import numpy as np
        N_NODES = 50000
        N_EDGES = 25000
        D_IN = 96
        D_OUT = 96
        N = feat.shape[0]
        ones = jnp.ones(src.shape[0], dtype=feat.dtype)
        out_deg = jax.ops.segment_sum(ones, src, num_segments=N)
        in_deg = jax.ops.segment_sum(ones, dst, num_segments=N)
        ci = jnp.clip(out_deg, 1.0, None) ** (-0.5)
        cj = jnp.clip(in_deg, 1.0, None) ** (-0.5)
        msg = feat[src] * ci[src, None]
        agg = jax.ops.segment_sum(msg, dst, num_segments=N) * cj[:, None]
        h = jnp.where(in_deg[:, None] > 0, agg, feat)
        return jnp.matmul(h, weight) + bias

    def _L1_gnn_ref(x, edge_index, edge_attr, W1, b1, W2, b2, Ws, bs, Wn, bn):
        import jax, jax.numpy as jnp
        import numpy as np
        N = 50000
        E = 25000
        D = 96
        ED = 17
        src, dst = (edge_index[0], edge_index[1])
        h = jax.nn.relu(edge_attr @ W1.T + b1)
        w = h @ W2.T + b2
        msg = w * x[src]
        agg = jax.ops.segment_sum(msg, dst, num_segments=x.shape[0])
        return jax.nn.relu(x @ Ws.T + bs + agg @ Wn.T + bn)
    edge_index = jnp.stack([src, dst])
    x = _layernorm(x + _L0_gnn_ref(x, L0_gnn_weight, L0_gnn_bias, src, dst), axis=-1)
    x = _layernorm(x + _L1_gnn_ref(x, edge_index, edge_attr_17, L1_gnn_W1, L1_gnn_b1, L1_gnn_W2, L1_gnn_b2, L1_gnn_Ws, L1_gnn_bs, L1_gnn_Wn, L1_gnn_bn), axis=-1)
    return x

_drawn_inputs = setup_inputs


def setup_inputs(seed=0):
    import zlib

    import numpy as np

    out = dict(_drawn_inputs(seed))
    spreads = {'L0_gnn_bias': (0.0, 0.1)}
    factors = {}
    for name, (base, spread) in spreads.items():
        noise = np.random.default_rng([zlib.crc32(name.encode()), seed]).standard_normal(out[name].shape)
        drawn = base * np.exp(spread * noise) if base else spread * noise
        out[name] = jnp.asarray(drawn.astype(out[name].dtype))
    for name, factor in factors.items():
        out[name] = (out[name] * factor).astype(out[name].dtype)
    return out
```

```python
from contextlib import ExitStack

import concourse.bass as bass
from concourse import mybir

NODES, D, EDGES, ED = 3125, 96, 103125, 17
P = 128
NT = -(-NODES // P)
NP = NT * P
DE = D + 1
CH = 8
SG = CH * P
NS = -(-EDGES // SG)
NC = NS * CH
NG = 2
GC = CH // NG
W0, W1 = 20, 48
KEYS = W0 * NT
B0 = 4
NB = NS // B0
VC = NG * W0
DVE_LOWS = 6
LO = 64
HI = NP // LO
PAD_DST, PAD_SRC = 4095, NP - 1
SWEEPS0, SWEEPS1 = -(-NP // W0) + 1, -(-NP // W1) + 1
BT = 5
TB = NT // BT
EPS = 1e-5


def build(nc, x_rows, x_cols, src_pm, dst_pm, dst_rows, ea_cols, w0e, b0, w1t, b1c, w2e, wse, wne, out):
    fp32, bf16, fp16, i32 = mybir.dt.float32, mybir.dt.bfloat16, mybir.dt.float16, mybir.dt.int32
    ALU, ACT, AX = mybir.AluOpType, mybir.ActivationFunctionType, mybir.AxisListType

    x1_table = nc.dram_tensor("x1_table", (NP, D), fp32, kind="Internal").ap()

    with ExitStack() as ctx:
        def sb(name, shape, dt):
            return ctx.enter_context(nc.sbuf_tensor(name, shape, dt))

        def sem(name):
            return ctx.enter_context(nc.semaphore(name))

        src_i = sb("src_i", [P, NC], i32)
        dst_i = sb("dst_i", [P, NC], i32)
        x_sb = sb("x_sb", [P, NT, D], fp32)
        xT = sb("xT", [D, NP], fp32)
        w0_sb = sb("w0_sb", [DE, DE], fp32)
        b0_sb = sb("b0_sb", [P, D], fp32)
        w1_sb = sb("w1_sb", [ED, D], fp32)
        b1_sb = sb("b1_sb", [D, 1], fp32)
        w2_sb = sb("w2_sb", [DE, D], fp32)
        ws_sb = sb("ws_sb", [DE, D], fp32)
        wn_sb = sb("wn_sb", [DE, D], fp32)
        iota_key = sb("iota_key", [P, NT, W0], fp16)
        iota_row = sb("iota_row", [P, P], fp16)
        iota_neg = sb("iota_neg", [P, P], fp16)
        iota_lo = sb("iota_lo", [P, LO, CH], bf16)
        iota_w1 = sb("iota_w1", [P, W1], fp32)
        iota_sw = sb("iota_sw", [1, SWEEPS0 + SWEEPS1], fp32)
        ident = sb("ident", [P, P], fp32)
        ones = sb("ones", [P, P], fp32)
        zeros = sb("zeros", [P, LO], bf16)
        part_i = sb("part_i", [P, 4, NC], i32)
        low6 = sb("low6", [P, NC], bf16)
        high6 = sb("high6", [P, NC], bf16)
        key_low = sb("key_low", [P, NC, 2], fp32)
        rel1 = sb("rel1", [P, NC], fp32)
        stats = sb("stats", [NS, 12], fp32)
        base0_f = sb("base0_f", [1, NS, NG], fp32)
        base1_f = sb("base1_f", [1, NS], fp32)
        base0_c = sb("base0_c", [1, NS * NG], fp32)
        base1_c = sb("base1_c", [1, NS], fp32)
        base0_i = sb("base0_i", [1, NS * NG], i32)
        base1_i = sb("base1_i", [1, NS], i32)
        spans = sb("spans", [1, 2], fp32)
        within = sb("within", [1, SWEEPS0 + SWEEPS1], fp32)
        sweeps_f = sb("sweeps_f", [1, 2], fp32)
        sweeps_i = sb("sweeps_i", [1, 2], i32)
        deg = sb("deg", [P, 6, NT], fp32)
        xs_part = sb("xs_part", [P, 3, NT, DE], bf16)
        xw = sb("xw", [P, NT, D], fp32)
        agg0T = sb("agg0T", [DE, NP + W0], fp32)
        x1 = sb("x1", [P, NT, D], fp32)
        bn6 = sb("bn6", [P, NT, 6], fp32)
        mv = sb("mv", [P, NT, 2], fp32)
        x1T = sb("x1T", [DE, NP], fp32)
        agg1T = sb("agg1T", [DE, NP + W1], fp32)
        lo_hot = sb("lo_hot", [P, 2, LO, CH], bf16)
        hi_hot = sb("hi_hot", [P, 2, HI, CH], bf16)
        scal = sb("scal", [P, B0, CH, 2], fp32)
        low_hot = sb("low_hot", [P, B0, CH, P], bf16)
        away = sb("away", [P, CH - DVE_LOWS, P], fp16)
        key_hot = sb("key_hot", [P, B0, CH, KEYS], bf16)
        counts = sb("counts", [P, NT, B0 * VC], fp16)
        window_sums = sb("window_sums", [DE, B0 * VC], fp32)
        room = key_hot[:, :, :, :].rearrange("p a b c -> p (a b c)").bitcast(fp32)
        used = [0]

        def inside(n, rows=P):
            used[0] += n
            assert used[0] <= B0 * CH * KEYS // 2
            return room[0:rows, used[0] - n:used[0]]

        masked = inside(SG, NS)
        diag = inside(5 * NS, NS).rearrange("p (a b) -> p a b", a=5)
        dst_r = inside(SG, NS).bitcast(i32)
        xs = inside(NT * D).rearrange("p (t d) -> p t d", t=NT)
        used[0] = 0
        gathered = [inside(CH * D).rearrange("p (c d) -> p c d", c=CH) for _ in range(2)]
        messages = [inside(CH * D).rearrange("p (c d) -> p c d", c=CH) for _ in range(2)]
        dst_hot = [inside(CH * W1).rearrange("p (c w) -> p c w", c=CH) for _ in range(2)]
        y = inside(NT * D).rearrange("p (t d) -> p t d", t=NT)
        ea_sb = sb("ea_sb", [ED, 2, SG], fp32)
        hidden = sb("hidden", [DE, 2, SG], fp32)
        index = sb("index", [P, 2, CH], i32)

        bank = [ctx.enter_context(nc.psum_tensor(f"bank{i}", [P, 512], fp32)) for i in range(8)]

        edges_in, nodes_in, weights_in = sem("edges_in"), sem("nodes_in"), sem("weights_in")
        const_ready, ident_zero = sem("const_ready"), sem("ident_zero")
        v_step, sweep_step, fold_step = sem("v_step"), sem("sweep_step"), sem("fold_step")
        carrier = sem("carrier")
        xw_made, xw_taken = sem("xw_made"), sem("xw_taken")
        diag_ready, bases_spread, sweeps_ready = sem("diag_ready"), sem("bases_spread"), sem("sweeps_ready")
        hist_ready, hist_used, hist_done = sem("hist_ready"), sem("hist_used"), sem("hist_done")
        deg_ready, root_ready = sem("deg_ready"), sem("root_ready")
        xs_ready = sem("xs_ready")
        scal_ready, keys_ready, lows_away, lows_ready, ring_used = (
            sem("scal_ready"), sem("keys_ready"), sem("lows_away"), sem("lows_ready"), sem("ring_used"))
        counts_made = [sem(f"counts_made{i}") for i in range(4)]
        counts_taken = [sem(f"counts_taken{i}") for i in range(4)]
        sums_made, sums_taken, window_added = sem("sums_made"), sem("sums_taken"), sem("window_added")
        bases0_ready, bases0_used, bases1_ready = sem("bases0_ready"), sem("bases0_used"), sem("bases1_ready")
        layer0_done = sem("layer0_done")
        indeg_made, agg_made = sem("indeg_made"), sem("agg_made")
        var_ready, std_ready = sem("var_ready"), sem("std_ready")
        x1_ready, x1_stored = sem("x1_ready"), sem("x1_stored")
        turned, turn_taken = sem("turned"), sem("turn_taken")
        attrs_in = [sem(f"attrs_in{i}") for i in range(2)]
        index_in = [sem(f"index_in{i}") for i in range(2)]
        rows_in = [sem(f"rows_in{i}") for i in range(2)]
        hidden_made, hidden_ready = sem("hidden_made"), sem("hidden_ready")
        weights_made, messages_ready = sem("weights_made"), sem("messages_ready")
        hot_ready, window_made, window_taken = sem("hot_ready"), sem("window_made"), sem("window_taken")
        layer1_done, self_made = sem("layer1_done"), sem("self_made")
        y_ready, out_stored = sem("y_ready"), sem("out_stored")

        def counter(engine, own):
            total = [0]

            def step():
                total[0] += 1
                return 1

            return step, lambda: engine.wait_ge(own, total[0])

        CONSTS = 16
        per_slot = (NS - NS // 2, NS // 2)

        block = ctx.enter_context(nc.Block())

        @block.sync
        def _(sp):
            sp.dma_start(dst_r, dst_rows).then_inc(edges_in, 16)
            sp.dma_start(src_i[:, :], src_pm).then_inc(edges_in, 16)
            sp.dma_start(dst_i[:, :], dst_pm).then_inc(edges_in, 16)
            for tile, source in ((w0_sb, w0e), (w1_sb, w1t), (b1_sb, b1c), (w2_sb, w2e), (ws_sb, wse), (wn_sb, wne)):
                sp.dma_start(tile[:, :], source).then_inc(weights_in, 16)
            sp.dma_start(b0_sb[:, :], b0.broadcast_to([P, D])).then_inc(weights_in, 16)
            sp.dma_start(xT[:, :], x_cols).then_inc(weights_in, 16)
            sp.dma_start(x_sb[:, :, :], x_rows.rearrange("(t p) d -> p t d", p=P)).then_inc(nodes_in, 16)

            sp.wait_ge(x1_ready, 1)
            sp.dma_start(x1_table.rearrange("(t p) d -> p t d", p=P), x1[:, :, :]).then_inc(x1_stored, 16)

            n_sweeps = sp.value_load(sweeps_i[0:1, 1:2], min_val=1, max_val=SWEEPS1)

            def load(sweep, i, slot):
                n = sweep * NS + i
                sp.wait_ge(hidden_ready, n * 2 + 2)
                sp.dma_start(ea_sb[:, slot, :], ea_cols[:, bass.ds(i * SG, SG)]).then_inc(attrs_in[slot], 16)
                sp.wait_ge(messages_ready, n * 2 + 2)
                sp.dma_start(index[:, slot, :], src_pm[:, bass.ds(i * CH, CH)]).then_inc(index_in[slot], 16)

            with sp.Fori(0, n_sweeps) as sweep:
                with sp.Fori(0, NS - 1, 2) as i:
                    load(sweep, i, 0)
                    load(sweep, i + 1, 1)
                load(sweep, NS - 1, 0)

            sp.wait_ge(y_ready, 1)
            full = NODES // P
            sp.dma_start(out[0:full * P, :].rearrange("(t p) d -> p t d", p=P), y[:, 0:full, :]).then_inc(out_stored, 16)
            sp.dma_start(out[full * P:NODES, :], y[0:NODES - full * P, full, :]).then_inc(out_stored, 16)
            sp.wait_ge(out_stored, 32)

        @block.gpsimd
        def _(pool):
            def numbers(tile, pattern):
                return pool.iota(tile, pattern, base=0, channel_multiplier=0, allow_small_or_imprecise_dtypes=True)

            pool.memset(ident[:, :], 0.0).then_inc(ident_zero, 1)
            pool.memset(ones[:, :], 1.0).then_inc(const_ready, 1)
            pool.wait_ge(ident_zero, 1)
            pool.affine_select(out=ident[:, :], in_=ident[:, :], compare_op=ALU.not_equal, fill=1.0, base=0,
                               pattern=[[-1, P]], channel_multiplier=1).then_inc(const_ready, 1)
            numbers(iota_lo[:, :, :], [[1, LO], [0, CH]]).then_inc(const_ready, 1)
            pool.memset(zeros[:, :], 0.0).then_inc(const_ready, 1)
            numbers(iota_sw[:, 0:SWEEPS0], [[W0, SWEEPS0]]).then_inc(const_ready, 1)
            numbers(iota_sw[:, SWEEPS0:], [[W1, SWEEPS1]]).then_inc(const_ready, 1)
            numbers(iota_key[:, :, :], [[1, NT], [NT, W0]]).then_inc(const_ready, 1)
            numbers(iota_row[:, :], [[1, P]]).then_inc(const_ready, 1)
            numbers(iota_neg[:, :], [[-1, P]]).then_inc(const_ready, 1)
            numbers(iota_w1[:, :], [[1, W1]]).then_inc(const_ready, 1)
            pool.memset(agg0T[:, :], 0.0).then_inc(const_ready, 1)
            pool.memset(agg1T[0:D, :], 0.0).then_inc(const_ready, 1)
            pool.memset(xs_part[:, :, :, D:DE], 0.0).then_inc(const_ready, 1)
            pool.wait_ge(const_ready, CONSTS)

            pool.wait_ge(sweeps_ready, 1)
            n_sweeps = pool.value_load(sweeps_i[0:1, 0:1], min_val=1, max_val=SWEEPS0)
            pool.sem_inc(window_added, 1)
            pool.sem_inc(bases0_used, 1)

            def add_windows(sweep, b, supers):
                first_window = sweep * (NS * NG) + b * (B0 * NG)
                bases = [pool.value_load(base0_i[0:1, bass.ds(b * (B0 * NG) + g, 1)], min_val=0, max_val=NP)
                         for g in range(supers * NG)]
                pool.wait_ge(sums_taken, sweep * (NB + 1) + b + 2)
                pool.sem_inc(carrier, 1)
                for g in range(supers * NG):
                    pool.wait_ge(window_added, first_window + g + 1)
                    pool.sem_inc(carrier, 1)
                    window = agg0T[:, bass.ds(bases[g], W0)]
                    pool.tensor_tensor(out=window, in0=window, in1=window_sums[:, g * W0:(g + 1) * W0],
                                       op=ALU.add).then_inc(window_added, 1)

            with pool.Fori(0, n_sweeps) as sweep:
                pool.wait_ge(bases0_ready, sweep + 1)
                pool.sem_inc(carrier, 1)
                with pool.Fori(0, NB) as b:
                    add_windows(sweep, b, B0)
                add_windows(sweep, NB, NS - NB * B0)
                pool.sem_inc(bases0_used, 1)
            pool.wait_ge(window_added, n_sweeps * (NS * NG) + 1)
            pool.sem_inc(layer0_done, 1)

            n_sweeps = pool.value_load(sweeps_i[0:1, 1:2], min_val=1, max_val=SWEEPS1)
            pool.wait_ge(x1_stored, 16)

            def gather(sweep, i, slot, nth):
                pool.wait_ge(messages_ready, (sweep * NS + i) * 2 + 2)
                pool.sem_inc(carrier, 1)
                pool.wait_ge(index_in[slot], (nth + 1) * 16)
                pool.sem_inc(carrier, 1)
                for c in range(CH):
                    pool.indirect_dma_start(out=gathered[slot][:, c, :], out_offset=None, in_=x1_table,
                                            in_offset=bass.IndirectOffsetOnAxis(ap=index[:, slot, c:c + 1], axis=0),
                                            ).then_inc(rows_in[slot], 16)

            with pool.Fori(0, n_sweeps) as sweep:
                with pool.Fori(0, NS // 2) as k:
                    for slot in range(2):
                        gather(sweep, k * 2 + slot, slot, sweep * per_slot[slot] + k)
                gather(sweep, NS - 1, 0, sweep * per_slot[0] + NS // 2)

        @block.vector
        def _(ve):
            step, settle = counter(ve, v_step)

            for row in (agg1T[D:DE, :], x1T[D:DE, :], hidden[D:DE, :, :]):
                ve.memset(row, 1.0).then_inc(const_ready, 1)
            ve.wait_ge(edges_in, 48)
            per_group = dst_r.rearrange("p (g e) -> p g e", g=NG)
            ve.tensor_reduce(out=stats[:, 0:NG], in_=per_group, axis=AX.X, op=ALU.min).then_inc(v_step, step())
            ve.scalar_tensor_tensor(out=masked, in0=dst_r, scalar=float(NP), in1=dst_r, op0=ALU.is_lt,
                                    op1=ALU.mult).then_inc(v_step, step())
            settle()
            ve.tensor_reduce(out=stats[:, 4:4 + NG], in_=masked.rearrange("p (g e) -> p g e", g=NG), axis=AX.X,
                             op=ALU.max).then_inc(v_step, step())
            ve.tensor_scalar(out=stats[:, 0:NG], in0=stats[:, 0:NG], scalar1=float(NP), scalar2=None,
                             op0=ALU.min).then_inc(v_step, step())
            settle()
            ve.tensor_reduce(out=stats[:, NG:NG + 1], in_=stats[:, 0:NG], axis=AX.X, op=ALU.min).then_inc(v_step, step())
            ve.tensor_tensor(out=stats[:, 6:6 + NG], in0=stats[:, 4:4 + NG], in1=stats[:, 0:NG],
                             op=ALU.subtract).then_inc(v_step, step())
            ve.tensor_reduce(out=stats[:, 8:9], in_=stats[:, 4:4 + NG], axis=AX.X, op=ALU.max).then_inc(v_step, step())
            settle()
            ve.tensor_reduce(out=stats[:, 3:4], in_=stats[:, 6:6 + NG], axis=AX.X, op=ALU.max).then_inc(v_step, step())
            ve.tensor_tensor(out=stats[:, 4:5], in0=stats[:, 8:9], in1=stats[:, NG:NG + 1],
                             op=ALU.subtract).then_inc(v_step, step())
            settle()
            ve.wait_ge(const_ready, CONSTS)
            for col in range(5):
                made = ve.tensor_scalar(out=diag[:, col, :], in0=ident[0:NS, 0:NS], scalar1=stats[:, col:col + 1],
                                        scalar2=None, op0=ALU.mult)
            made.then_inc(diag_ready, 1)
            for n, (shift, mask) in enumerate(((7, None), (None, P - 1), (6, None), (None, LO - 1))):
                ve.tensor_scalar(out=part_i[:, n, :], in0=src_i[:, :], scalar1=mask if shift is None else shift, scalar2=None,
                                 op0=ALU.bitwise_and if shift is None else ALU.logical_shift_right).then_inc(v_step, step())
            settle()
            ve.tensor_copy(high6[:, :], part_i[:, 2, :]).then_inc(v_step, step())
            ve.tensor_copy(low6[:, :], part_i[:, 3, :]).then_inc(v_step, step())
            ve.tensor_scalar(out=key_low[:, :, 1], in0=part_i[:, 1, :], scalar1=-1.0, scalar2=None,
                             op0=ALU.mult).then_inc(v_step, step())
            ve.wait_ge(bases_spread, 1)
            spread = bank[0][:, 0:5 * NS].rearrange("p (a b) -> p a b", a=5)
            dst_g = dst_i[:, :].rearrange("p (s g c) -> p s g c", g=NG, c=GC)
            key_g = key_low[:, :, 0].rearrange("p (s g c) -> p s g c", g=NG, c=GC)
            for g in range(NG):
                ve.tensor_tensor(out=key_g[:, :, g, :], in0=dst_g[:, :, g, :],
                                 in1=spread[:, g, :].unsqueeze(2).broadcast_to([P, NS, GC]),
                                 op=ALU.subtract).then_inc(v_step, step())
            ve.tensor_tensor(out=rel1[:, :].rearrange("p (s c) -> p s c", c=CH),
                             in0=dst_i[:, :].rearrange("p (s c) -> p s c", c=CH),
                             in1=spread[:, NG, :].unsqueeze(2).broadcast_to([P, NS, CH]),
                             op=ALU.subtract).then_inc(v_step, step())
            for g in range(NG):
                ve.tensor_copy(base0_f[:, :, g], spread[0:1, g, :]).then_inc(v_step, step())
            ve.tensor_copy(base1_f[:, :], spread[0:1, NG, :]).then_inc(v_step, step())
            ve.tensor_reduce(out=spans[:, :], in_=spread[0:1, 3:5, :], axis=AX.X, op=ALU.max).then_inc(v_step, step())
            settle()
            ve.scalar_tensor_tensor(out=key_low[:, :, 0], in0=key_low[:, :, 0], scalar=float(NT), in1=part_i[:, 0, :],
                                    op0=ALU.mult, op1=ALU.add).then_inc(v_step, step())
            for n, (a, z) in enumerate(((0, SWEEPS0), (SWEEPS0, SWEEPS0 + SWEEPS1))):
                ve.tensor_scalar(out=within[:, a:z], in0=iota_sw[:, a:z], scalar1=spans[:, n:n + 1], scalar2=None,
                                 op0=ALU.is_le).then_inc(v_step, step())
            settle()
            for n, (a, z) in enumerate(((0, SWEEPS0), (SWEEPS0, SWEEPS0 + SWEEPS1))):
                ve.tensor_reduce(out=sweeps_f[:, n:n + 1], in_=within[:, a:z], axis=AX.X, op=ALU.add).then_inc(v_step, step())
            settle()
            ve.tensor_scalar(out=sweeps_i[:, :], in0=sweeps_f[:, :], scalar1=1.0, scalar2=None,
                             op0=ALU.max).then_inc(sweeps_ready, 1)

            def hist(s, slot):
                ve.wait_ge(hist_used, s + 1)
                for hot, width, part in ((lo_hot, LO, low6), (hi_hot, HI, high6)):
                    made = ve.tensor_tensor(
                        out=hot[:, slot, :, :], in0=iota_lo[:, 0:width, :],
                        in1=part[:, bass.ds(s * CH, CH)].unsqueeze(1).broadcast_to([P, width, CH]), op=ALU.is_equal)
                made.then_inc(hist_ready, 1)

            with ve.Fori(0, NS // 2) as k:
                hist(k * 2, 0)
                hist(k * 2 + 1, 1)
            hist(NS - 1, 0)

            ve.wait_ge(hist_done, 1)
            pairs = bank[1][0:LO, 0:HI].rearrange("p (t two) -> p t two", two=2)
            for half in range(2):
                ve.tensor_scalar(out=deg[half * LO:(half + 1) * LO, 0, :], in0=pairs[:, :, half], scalar1=1.0, scalar2=None,
                                 op0=ALU.max).then_inc(v_step, step())
            settle()
            ve.sem_inc(deg_ready, 1)

            def inverse_root(of, root, inv, tmp):
                ve.reciprocal(inv, root).then_inc(v_step, step())
                settle()
                ve.tensor_tensor(out=tmp, in0=inv, in1=inv, op=ALU.mult).then_inc(v_step, step())
                settle()
                ve.tensor_tensor(out=tmp, in0=tmp, in1=of, op=ALU.mult).then_inc(v_step, step())
                settle()
                ve.tensor_scalar(out=tmp, in0=tmp, scalar1=-0.5, scalar2=1.5, op0=ALU.mult, op1=ALU.add).then_inc(v_step, step())
                settle()
                ve.tensor_tensor(out=inv, in0=inv, in1=tmp, op=ALU.mult).then_inc(v_step, step())
                settle()

            ve.wait_ge(root_ready, 1)
            inverse_root(deg[:, 0, :], deg[:, 1, :], deg[:, 2, :], deg[:, 3, :])
            ve.wait_ge(nodes_in, 16)
            ve.tensor_tensor(out=xs, in0=x_sb[:, :, :], in1=deg[:, 2, :].unsqueeze(2).broadcast_to([P, NT, D]),
                             op=ALU.mult).then_inc(v_step, step())
            settle()
            for part in range(3):
                ve.tensor_copy(xs_part[:, part, :, 0:D], xs).then_inc(v_step, step())
                settle()
                if part < 2:
                    ve.tensor_tensor(out=xs, in0=xs, in1=xs_part[:, part, :, 0:D], op=ALU.subtract).then_inc(v_step, step())
                    settle()
            ve.tensor_scalar(out=xs_part[:, 0, :, D:DE], in0=xs_part[:, 0, :, D:DE], scalar1=1.0, scalar2=None,
                             op0=ALU.add).then_inc(v_step, step())
            settle()
            ve.sem_inc(xs_ready, 1)

            ve.wait_ge(weights_in, 128)
            ve.tensor_tensor(out=x_sb[:, :, :], in0=x_sb[:, :, :], in1=b0_sb[:, :].unsqueeze(1).broadcast_to([P, NT, D]),
                             op=ALU.add).then_inc(v_step, step())

            n_sweeps = ve.value_load(sweeps_i[0:1, 0:1], min_val=1, max_val=SWEEPS0)

            def one_hots(sweep, s, q):
                n = sweep * NS + s
                ve.wait_ge(ring_used, n + 1)
                ve.tensor_copy(scal[:, q, :, :], key_low[:, bass.ds(s * CH, CH), :]).then_inc(scal_ready, 1)
                ve.wait_ge(scal_ready, n + 1)
                for c in range(CH):
                    ve.tensor_scalar(out=key_hot[:, q, c, :], in0=iota_key[:, :, :].rearrange("p a b -> p (a b)"),
                                     scalar1=scal[:, q, c, 0:1], scalar2=None, op0=ALU.is_equal)
                ve.tensor_tensor(out=low_hot[:, q, 0:DVE_LOWS, :],
                                 in0=iota_neg[:, :].unsqueeze(1).broadcast_to([P, DVE_LOWS, P]),
                                 in1=scal[:, q, 0:DVE_LOWS, 1:2].broadcast_to([P, DVE_LOWS, P]),
                                 op=ALU.is_equal).then_inc(keys_ready, 1)

            with ve.Fori(0, n_sweeps) as sweep:
                ve.wait_ge(bases0_used, sweep + 1)
                ve.wait_ge(ring_used, sweep * NS + B0)
                ve.tensor_scalar(out=base0_c[:, :], in0=base0_f[:, :, :].rearrange("p s g -> p (s g)"), scalar1=float(NP),
                                 scalar2=None, op0=ALU.min).then_inc(sweep_step, 1)
                ve.wait_ge(sweep_step, sweep * 3 + 1)
                ve.tensor_copy(base0_i[:, :], base0_c[:, :]).then_inc(bases0_ready, 1)
                with ve.Fori(0, NB) as b:
                    for q in range(B0):
                        one_hots(sweep, b * B0 + q, q)
                one_hots(sweep, NS - 1, 0)
                ve.wait_ge(keys_ready, (sweep + 1) * NS)
                ve.tensor_scalar(out=key_low[:, :, 0], in0=key_low[:, :, 0], scalar1=-float(KEYS), scalar2=None,
                                 op0=ALU.add).then_inc(sweep_step, 1)
                ve.tensor_scalar(out=base0_f[:, :, :], in0=base0_f[:, :, :], scalar1=float(W0), scalar2=None,
                                 op0=ALU.add).then_inc(sweep_step, 1)
                ve.wait_ge(sweep_step, sweep * 3 + 3)

            def norm(target, source):
                for t in range(NT):
                    ve.bn_stats(out=bn6[:, t, :], in_=source[:, t, :]).then_inc(v_step, step())
                settle()
                for t in range(NT):
                    ve.bn_aggr(out=mv[:, t, :], in_=bn6[:, t, :]).then_inc(v_step, step())
                settle()
                ve.tensor_scalar(out=deg[:, 0, :], in0=mv[:, :, 1], scalar1=EPS, scalar2=None, op0=ALU.add).then_inc(v_step, step())
                settle()
                ve.sem_inc(var_ready, 1)
                ve.wait_ge(std_ready, 1 if target is x1 else 2)
                inverse_root(deg[:, 0, :], deg[:, 1, :], deg[:, 2, :], deg[:, 3, :])
                for t in range(NT):
                    ve.tensor_scalar(out=target[:, t, :], in0=source[:, t, :], scalar1=mv[:, t, 0:1],
                                     scalar2=deg[:, 2, t:t + 1], op0=ALU.subtract, op1=ALU.mult).then_inc(v_step, step())
                settle()

            ve.wait_ge(indeg_made, 1)
            in_degree = bank[0][:, 0:NT]
            ve.tensor_scalar(out=deg[:, 4, :], in0=in_degree, scalar1=0.0, scalar2=None, op0=ALU.is_equal).then_inc(v_step, step())
            ve.tensor_scalar(out=deg[:, 0, :], in0=in_degree, scalar1=1.0, scalar2=None, op0=ALU.max).then_inc(v_step, step())
            settle()
            ve.sem_inc(deg_ready, 1)
            ve.wait_ge(xw_taken, TB)
            ve.tensor_tensor(out=xw[:, :, :], in0=xw[:, :, :], in1=deg[:, 4, :].unsqueeze(2).broadcast_to([P, NT, D]),
                             op=ALU.mult).then_inc(v_step, step())
            settle()
            ve.tensor_tensor(out=xw[:, :, :], in0=xw[:, :, :], in1=x_sb[:, :, :], op=ALU.add).then_inc(v_step, step())
            ve.wait_ge(root_ready, 2)
            inverse_root(deg[:, 0, :], deg[:, 1, :], deg[:, 2, :], deg[:, 3, :])
            for g in range(TB):
                tiles = slice(g * BT, (g + 1) * BT)
                ve.wait_ge(agg_made, g + 1)
                ve.tensor_tensor(out=x1[:, tiles, :], in0=bank[1 + g][:, 0:BT * D].rearrange("p (t d) -> p t d", t=BT),
                                 in1=deg[:, 2, tiles].unsqueeze(2).broadcast_to([P, BT, D]), op=ALU.mult).then_inc(v_step, step())
            settle()
            ve.tensor_tensor(out=xw[:, :, :], in0=xw[:, :, :], in1=x1[:, :, :], op=ALU.add).then_inc(v_step, step())
            settle()
            norm(x1, xw)
            ve.sem_inc(x1_ready, 1)

            n_sweeps = ve.value_load(sweeps_i[0:1, 1:2], min_val=1, max_val=SWEEPS1)
            ve.sem_inc(messages_ready, 4)
            ve.sem_inc(window_taken, 2)

            def fold(sweep, i, slot, nth):
                n = sweep * NS + i
                base = ve.value_load(base1_i[0:1, bass.ds(i, 1)], min_val=0, max_val=NP)
                ve.wait_ge(window_made, n + 1)
                ve.tensor_tensor(out=dst_hot[slot], in0=iota_w1[:, :].unsqueeze(1).broadcast_to([P, CH, W1]),
                                 in1=rel1[:, bass.ds(i * CH, CH)].unsqueeze(2).broadcast_to([P, CH, W1]),
                                 op=ALU.is_equal).then_inc(hot_ready, 1)
                ve.wait_ge(rows_in[slot], (nth + 1) * (CH * 16))
                for h in range(2):
                    ve.wait_ge(weights_made, n * 2 + h + 5)
                    half = slice(h * CH // 2, (h + 1) * CH // 2)
                    ve.tensor_tensor(out=messages[slot][:, half, :],
                                     in0=bank[2 + 2 * slot + h][:, 0:CH // 2 * D].rearrange("p (c d) -> p c d", d=D),
                                     in1=gathered[slot][:, half, :], op=ALU.mult).then_inc(messages_ready, 1)
                ve.wait_ge(window_made, n + 3)
                ve.wait_ge(window_taken, n + 2)
                window = agg1T[0:D, bass.ds(base, W1)]
                ve.tensor_tensor(out=window, in0=window, in1=bank[6 + slot][0:D, 0:W1], op=ALU.add).then_inc(window_taken, 1)

            with ve.Fori(0, n_sweeps) as sweep:
                ve.wait_ge(window_made, sweep * NS + 2)
                ve.tensor_scalar(out=base1_c[:, :], in0=base1_f[:, :], scalar1=float(NP), scalar2=None,
                                 op0=ALU.min).then_inc(fold_step, 1)
                ve.wait_ge(fold_step, sweep * 4 + 1)
                ve.tensor_copy(base1_i[:, :], base1_c[:, :]).then_inc(fold_step, 1)
                ve.wait_ge(fold_step, sweep * 4 + 2)
                ve.sem_inc(carrier, 1)
                with ve.Fori(0, NS // 2) as k:
                    for slot in range(2):
                        fold(sweep, k * 2 + slot, slot, sweep * per_slot[slot] + k)
                fold(sweep, NS - 1, 0, sweep * per_slot[0] + NS // 2)
                ve.wait_ge(hot_ready, (sweep + 1) * NS)
                ve.tensor_scalar(out=rel1[:, :], in0=rel1[:, :], scalar1=-float(W1), scalar2=None,
                                 op0=ALU.add).then_inc(fold_step, 1)
                ve.tensor_scalar(out=base1_f[:, :], in0=base1_f[:, :], scalar1=float(W1), scalar2=None,
                                 op0=ALU.add).then_inc(fold_step, 1)
                ve.wait_ge(fold_step, sweep * 4 + 4)
            ve.wait_ge(window_taken, n_sweeps * NS + 2)
            ve.sem_inc(layer1_done, 1)

            for g in range(TB):
                ve.wait_ge(self_made, g + 1)
                ve.scalar_tensor_tensor(
                    out=xw[:, g * BT:(g + 1) * BT, :], in0=bank[g][:, 0:BT * D].rearrange("p (t d) -> p t d", t=BT), scalar=0.0,
                    in1=x1[:, g * BT:(g + 1) * BT, :], op0=ALU.max, op1=ALU.add).then_inc(v_step, step())
            settle()
            norm(y, xw)
            ve.sem_inc(y_ready, 1)

        @block.scalar
        def _(ac):
            for g in range(TB):
                ac.wait_ge(xw_made, g + 1)
                ac.activation(xw[:, g * BT:(g + 1) * BT, :], bank[2 + g][:, 0:BT * D].rearrange("p (t d) -> p t d", t=BT),
                              ACT.Copy).then_inc(xw_taken, 1)
            ac.wait_ge(deg_ready, 1)
            ac.activation(deg[:, 1, :], deg[:, 0, :], ACT.Sqrt).then_inc(root_ready, 1)

            ac.wait_ge(sweeps_ready, 1)
            n_sweeps = ac.value_load(sweeps_i[0:1, 0:1], min_val=1, max_val=SWEEPS0)
            for taken in counts_taken:
                ac.sem_inc(taken, 1)
            ac.sem_inc(sums_taken, 1)

            def lows(sweep, s, q):
                n = sweep * NS + s
                ac.wait_ge(scal_ready, n + 1)
                ac.wait_ge(ring_used, n + 1)
                ac.wait_ge(lows_ready, n + 1)
                for c in range(DVE_LOWS, CH):
                    ac.activation(away[:, c - DVE_LOWS, :], iota_row[:, :], ACT.Abs,
                                  bias=scal[:, q, c, 1:2]).then_inc(lows_away, 1)
                ac.wait_ge(lows_away, (n + 1) * (CH - DVE_LOWS))
                ac.activation(low_hot[:, q, DVE_LOWS:CH, :], away[:, :, :], ACT.Relu, bias=1.0,
                              scale=-1.0).then_inc(lows_ready, 1)

            def take_counts(sweep, b, q):
                for g in range(NG):
                    k = (q % 2) * 2 + g
                    nth = sweep * per_slot[q % 2] + b * 2 + q // 2
                    ac.wait_ge(counts_made[k], nth + 1)
                    ac.activation(counts[:, :, q * VC + g * W0:q * VC + (g + 1) * W0],
                                  bank[k][:, 0:KEYS].rearrange("p (a b) -> p a b", a=NT), ACT.Copy).then_inc(counts_taken[k], 1)

            def take_sums(sweep, b, supers):
                ac.wait_ge(sums_made, sweep * (NB + 1) + b + 1)
                ac.wait_ge(window_added, sweep * (NS * NG) + b * (B0 * NG) + 1)
                ac.activation(window_sums[:, 0:supers * VC], bank[4][0:DE, 0:supers * VC], ACT.Copy).then_inc(sums_taken, 1)

            ac.sem_inc(lows_ready, 1)
            with ac.Fori(0, n_sweeps) as sweep:
                ac.wait_ge(ring_used, sweep * NS + B0)
                lows(sweep, 0, 0)
                with ac.Fori(0, NB) as b:
                    for q in range(B0):
                        lows(sweep, b * B0 + q + 1, (q + 1) % B0)
                        take_counts(sweep, b, q)
                    take_sums(sweep, b, B0)
                take_counts(sweep, NB, 0)
                take_sums(sweep, NB, NS - NB * B0)

            ac.wait_ge(deg_ready, 2)
            ac.activation(deg[:, 1, :], deg[:, 0, :], ACT.Sqrt).then_inc(root_ready, 1)
            ac.wait_ge(var_ready, 1)
            ac.activation(deg[:, 1, :], deg[:, 0, :], ACT.Sqrt).then_inc(std_ready, 1)

            for k in range(-(-NT // 4)):
                tiles = min(4, NT - k * 4)
                ac.wait_ge(turned, k + 1)
                ac.activation(x1T[0:D, k * 4 * P:(k * 4 + tiles) * P], bank[k][0:D, 0:tiles * P], ACT.Copy).then_inc(turn_taken, 1)

            n_sweeps = ac.value_load(sweeps_i[0:1, 1:2], min_val=1, max_val=SWEEPS1)
            ac.sem_inc(hidden_ready, 4)

            def rectify(sweep, i, slot):
                n = sweep * NS + i
                ac.wait_ge(weights_made, n * 2 + 2)
                for h in range(2):
                    ac.wait_ge(hidden_made, n * 2 + h + 1)
                    ac.activation(hidden[0:D, slot, h * 512:(h + 1) * 512], bank[h][0:D, :], ACT.Relu,
                                  bias=b1_sb[:, 0:1]).then_inc(hidden_ready, 1)

            with ac.Fori(0, n_sweeps) as sweep:
                with ac.Fori(0, NS - 1, 2) as i:
                    rectify(sweep, i, 0)
                    rectify(sweep, i + 1, 1)
                rectify(sweep, NS - 1, 0)
            ac.wait_ge(var_ready, 2)
            ac.activation(deg[:, 1, :], deg[:, 0, :], ACT.Sqrt).then_inc(std_ready, 1)

        @block.tensor
        def _(te):
            te.wait_ge(const_ready, CONSTS)
            te.wait_ge(diag_ready, 1)
            te.matmul(bank[0][:, 0:5 * NS], ones[0:NS, :], diag.rearrange("p a b -> p (a b)"), start=True,
                      stop=True).then_inc(bases_spread, 1)
            te.wait_ge(weights_in, 128)
            for g in range(TB):
                for t in range(BT):
                    at = (g * BT + t) * P
                    made = te.matmul(bank[2 + g][:, t * D:(t + 1) * D], xT[:, at:at + P], w0_sb[0:D, 0:D], start=True, stop=True)
                made.then_inc(xw_made, 1)

            te.sem_inc(hist_used, 2)
            tally = bank[1][0:LO, 0:HI]
            te.matmul(tally, zeros[:, 0:LO], zeros[:, 0:HI], start=True, stop=False)

            def hist(s, slot):
                te.wait_ge(hist_ready, s + 1)
                for c in range(CH):
                    made = te.matmul(tally, lo_hot[:, slot, :, c], hi_hot[:, slot, :, c], start=False, stop=False)
                made.then_inc(hist_used, 1)

            with te.Fori(0, NS // 2) as k:
                hist(k * 2, 0)
                hist(k * 2 + 1, 1)
            hist(NS - 1, 0)
            te.matmul(tally, zeros[:, 0:LO], zeros[:, 0:HI], start=False, stop=True).then_inc(hist_done, 1)

            te.wait_ge(sweeps_ready, 1)
            n_sweeps = te.value_load(sweeps_i[0:1, 0:1], min_val=1, max_val=SWEEPS0)
            te.sem_inc(ring_used, B0)
            te.wait_ge(xw_taken, TB)

            def count(sweep, b, q):
                n = sweep * NS + b * B0 + q
                te.wait_ge(keys_ready, n + 1)
                te.wait_ge(lows_ready, n + 2)
                for g in range(NG):
                    k = (q % 2) * 2 + g
                    te.wait_ge(counts_taken[k], sweep * per_slot[q % 2] + b * 2 + q // 2 + 1)
                    for c in range(g * GC, (g + 1) * GC):
                        made = te.matmul(bank[k][:, 0:KEYS], low_hot[:, q, c, :], key_hot[:, q, c, :],
                                         start=c == g * GC, stop=c == (g + 1) * GC - 1)
                    made.then_inc(counts_made[k], 1)
                te.wait_ge(counts_made[k], sweep * per_slot[q % 2] + b * 2 + q // 2 + 1)
                te.sem_inc(ring_used, 1)

            def sums(sweep, b, supers):
                for k in range(4):
                    last = b * 2 + (supers + 1 - k // 2) // 2 - 1
                    te.wait_ge(counts_taken[k], sweep * per_slot[k // 2] + last + 2)
                te.wait_ge(sums_taken, sweep * (NB + 1) + b + 1)
                for a in range(NT):
                    for part in range(3):
                        made = te.matmul(bank[4][0:DE, 0:supers * VC], xs_part[:, part, a, :], counts[:, a, 0:supers * VC],
                                         start=a == part == 0, stop=a == NT - 1 and part == 2)
                made.then_inc(sums_made, 1)

            with te.Fori(0, n_sweeps) as sweep:
                with te.Fori(0, NB) as b:
                    for q in range(B0):
                        count(sweep, b, q)
                    te.wait_ge(xs_ready, 1)
                    sums(sweep, b, B0)
                count(sweep, NB, 0)
                sums(sweep, NB, NS - NB * B0)

            te.wait_ge(layer0_done, 1)
            for t in range(NT):
                made = te.matmul(bank[0][:, t:t + 1], agg0T[:, t * P:(t + 1) * P], w0_sb[:, D:DE], start=True, stop=True)
            made.then_inc(indeg_made, 1)
            for g in range(TB):
                for t in range(BT):
                    at = (g * BT + t) * P
                    made = te.matmul(bank[1 + g][:, t * D:(t + 1) * D], agg0T[0:D, at:at + P], w0_sb[0:D, 0:D], start=True, stop=True)
                made.then_inc(agg_made, 1)

            te.wait_ge(x1_ready, 1)
            for k in range(-(-NT // 4)):
                tiles = min(4, NT - k * 4)
                for t in range(tiles):
                    made = te.transpose(bank[k][0:D, t * P:(t + 1) * P], x1[:, k * 4 + t, :], ident[:, :])
                made.then_inc(turned, 1)

            n_sweeps = te.value_load(sweeps_i[0:1, 1:2], min_val=1, max_val=SWEEPS1)
            te.sem_inc(weights_made, 4)
            te.sem_inc(window_made, 2)
            te.wait_ge(turn_taken, -(-NT // 4))

            def edges(sweep, i, slot, nth):
                n = sweep * NS + i
                te.wait_ge(attrs_in[slot], (nth + 1) * 16)
                for h in range(2):
                    te.wait_ge(hidden_ready, n * 2 + h + 3)
                    te.matmul(bank[h][0:D, :], w1_sb[:, :], ea_sb[:, slot, h * 512:(h + 1) * 512], start=True,
                              stop=True).then_inc(hidden_made, 1)
                for h in range(2):
                    te.wait_ge(hidden_ready, n * 2 + h + 5)
                    te.wait_ge(messages_ready, n * 2 + h + 1)
                    for c in range(CH // 2):
                        at = h * 512 + c * P
                        made = te.matmul(bank[2 + 2 * slot + h][:, c * D:(c + 1) * D], hidden[:, slot, at:at + P], w2_sb[:, :],
                                         start=True, stop=True)
                    made.then_inc(weights_made, 1)
                te.wait_ge(hot_ready, n + 1)
                te.wait_ge(window_taken, n + 1)
                te.wait_ge(messages_ready, n * 2 + 6)
                for c in range(CH):
                    made = te.matmul(bank[6 + slot][0:D, 0:W1], messages[slot][:, c, :], dst_hot[slot][:, c, :],
                                     start=c == 0, stop=c == CH - 1)
                made.then_inc(window_made, 1)

            with te.Fori(0, n_sweeps) as sweep:
                with te.Fori(0, NS // 2) as k:
                    for slot in range(2):
                        edges(sweep, k * 2 + slot, slot, sweep * per_slot[slot] + k)
                edges(sweep, NS - 1, 0, sweep * per_slot[0] + NS // 2)

            te.wait_ge(layer1_done, 1)
            for g in range(TB):
                for t in range(BT):
                    at = (g * BT + t) * P
                    into = bank[g][:, t * D:(t + 1) * D]
                    te.matmul(into, x1T[:, at:at + P], ws_sb[:, :], start=True, stop=False)
                    made = te.matmul(into, agg1T[:, at:at + P], wn_sb[:, :], start=False, stop=True)
                made.then_inc(self_made, 1)


def kernel(x, src, dst, edge_attr_17, L0_gnn_weight, L0_gnn_bias, L1_gnn_W1, L1_gnn_b1, L1_gnn_W2, L1_gnn_b2,
           L1_gnn_Ws, L1_gnn_bs, L1_gnn_Wn, L1_gnn_bn):
    import numpy as np
    import concourse.bacc as bacc
    from concourse.bass_utils import run_bass_kernel_spmd

    def padded(a, shape, fill=0):
        a = np.asarray(a)
        whole = np.full(shape, fill, a.dtype)
        whole[tuple(slice(0, n) for n in a.shape)] = a
        return whole

    x = np.asarray(x)
    src_pad, dst_pad = padded(src, (NC * P,), PAD_SRC), padded(dst, (NC * P,), PAD_DST)
    weight = padded(L0_gnn_weight, (DE, DE))
    weight[D, D] = 1
    x_pad = padded(x, (NP, D))

    def with_bias(w, b):
        return np.concatenate([np.asarray(w).T, np.asarray(b)[None]])

    arrays = {
        "x_rows": x_pad,
        "x_cols": x_pad.T,
        "src_pm": src_pad.reshape(NC, P).T,
        "dst_pm": dst_pad.reshape(NC, P).T,
        "dst_rows": dst_pad.reshape(NS, SG),
        "ea_cols": padded(edge_attr_17, (NC * P, ED)).T,
        "w0e": weight,
        "b0": np.asarray(L0_gnn_bias)[None],
        "w1t": np.asarray(L1_gnn_W1).T,
        "b1c": np.asarray(L1_gnn_b1)[:, None],
        "w2e": with_bias(L1_gnn_W2, L1_gnn_b2),
        "wse": with_bias(L1_gnn_Ws, L1_gnn_bs),
        "wne": with_bias(L1_gnn_Wn, L1_gnn_bn),
    }
    arrays = {name: np.ascontiguousarray(a) for name, a in arrays.items()}
    nc = bacc.Bacc("TRN2", target_bir_lowering=False, num_devices=1)
    args = [nc.dram_tensor(name, a.shape, mybir.dt.from_np(a.dtype), kind="ExternalInput").ap() for name, a in arrays.items()]
    out = nc.dram_tensor("out", (NODES, D), mybir.dt.float32, kind="ExternalOutput").ap()
    build(nc, *args, out)
    return run_bass_kernel_spmd(nc, [arrays], core_ids=[0]).results[0]["out"]
```

```python
from contextlib import ExitStack

import concourse.bass as bass
from concourse import mybir

NODES, D, EDGES, ED = 3125, 96, 103125, 17
P = 128
NT = -(-NODES // P)
NP = NT * P
DE = D + 1
CH = 8
SG = CH * P
NS = -(-EDGES // SG)
NC = NS * CH
NG = 4
GC = CH // NG
W0, W1 = 12, 48
KEYS = W0 * NT
B0 = 4
NB = NS // B0
VC = NG * W0
DVE_LOWS = 5
LO = 64
HI = NP // LO
PAD_DST, PAD_SRC = 4095, NP - 1
SLOTS = 4
SWEEPS0, SWEEPS1 = -(-NP // W0) + 1, -(-NP // W1) + 1
BT = 5
TB = NT // BT
EPS = 1e-5
ROW_PARTS = (1, 1, 1, 2, 2, 3, 3)
W_PARTS = ((1, 2, 3, 1, 2, 1, 2), (0, 0, 0, 3, 0, 3, 0))
RK = ED * len(ROW_PARTS)


def build(nc, x_rows, x_cols, src_pm, dst_pm, dst_rows, ea_cols, w0e, b0, w1t, b1c, w2e, wse, wnt, part_masks, out):
    fp32, bf16, fp16, i32 = mybir.dt.float32, mybir.dt.bfloat16, mybir.dt.float16, mybir.dt.int32
    ALU, ACT, AX = mybir.AluOpType, mybir.ActivationFunctionType, mybir.AxisListType

    x1_table = nc.dram_tensor("x1_table", (NP, D), fp32, kind="Internal").ap()

    with ExitStack() as ctx:
        def sb(name, shape, dt):
            return ctx.enter_context(nc.sbuf_tensor(name, shape, dt))

        def sem(name):
            return ctx.enter_context(nc.semaphore(name))

        src_i = sb("src_i", [P, NC], i32)
        dst_i = sb("dst_i", [P, NC], i32)
        x_sb = sb("x_sb", [P, NT, D], fp32)
        w0_sb = sb("w0_sb", [DE, DE], fp32)
        b0_sb = sb("b0_sb", [P, D], fp32)
        w1_rep = sb("w1_rep", [RK, D], fp32)
        w1_sb = sb("w1_sb", [RK, 2, D], bf16)
        masks = sb("masks", [RK, 8], fp32)
        b1_sb = sb("b1_sb", [D, 1], fp32)
        w2_sb = sb("w2_sb", [DE, D], fp32)
        ws_sb = sb("ws_sb", [D + 2, D], fp32)
        wn_sb = sb("wn_sb", [D, D], fp32)
        iota_key = sb("iota_key", [P, NT, W0], fp16)
        iota_row = sb("iota_row", [P, P], fp16)
        iota_neg = sb("iota_neg", [P, P], fp16)
        iota_lo = sb("iota_lo", [P, LO, CH], bf16)
        iota_w1 = sb("iota_w1", [P, W1], fp32)
        iota_sw = sb("iota_sw", [1, SWEEPS0 + SWEEPS1], fp32)
        ident = sb("ident", [P, P], fp32)
        ones = sb("ones", [P, P], fp32)
        zeros = sb("zeros", [P, LO], bf16)
        low6 = sb("low6", [P, NC], bf16)
        high6 = sb("high6", [P, NC], bf16)
        key_low = sb("key_low", [P, NC, 2], fp32)
        rel1 = sb("rel1", [P, NC], fp32)
        stats = sb("stats", [NS, 16], fp32)
        base0_f = sb("base0_f", [1, NS, NG], fp32)
        base1_f = sb("base1_f", [1, NS], fp32)
        base0_c = sb("base0_c", [1, NS * NG], fp32)
        base1_c = sb("base1_c", [1, NS], fp32)
        base0_i = sb("base0_i", [1, NS * NG], i32)
        base1_i = sb("base1_i", [1, NS], i32)
        spans = sb("spans", [1, 2], fp32)
        within = sb("within", [1, SWEEPS0 + SWEEPS1], fp32)
        sweeps_f = sb("sweeps_f", [1, 2], fp32)
        sweeps_i = sb("sweeps_i", [1, 2], i32)
        deg = sb("deg", [P, 6, NT], fp32)
        xs_part = sb("xs_part", [P, 3, NT, DE], bf16)
        xw = sb("xw", [P, NT, D], fp32)
        agg0T = sb("agg0T", [DE, NP + W0], fp32)
        x1 = sb("x1", [P, NT, D], fp32)
        bn6 = sb("bn6", [P, NT, 6], fp32)
        norms = sb("norms", [P, 6, NT], fp32)
        y = sb("y", [P, NT, D], fp32)
        x1T = sb("x1T", [D + 2, NP], fp32)
        xT = x1T[0:D, :]
        agg1T = sb("agg1T", [D, NP + W1], fp32)
        lo_hot = sb("lo_hot", [P, 2, LO, CH], bf16)
        hi_hot = sb("hi_hot", [P, 2, HI, CH], bf16)
        scal = sb("scal", [P, B0, CH, 2], fp32)
        low_hot = sb("low_hot", [P, B0, CH, P], bf16)
        away = sb("away", [P, CH - DVE_LOWS, P], fp16)
        key_hot = sb("key_hot", [P, B0, CH, KEYS], bf16)
        counts_even = sb("counts", [P, NT, B0 * VC], fp16)
        window_sums = sb("window_sums", [DE, B0 * VC], fp32)
        masked = counts_even[0:NS, :, :].rearrange("p a b -> p (a b)").bitcast(fp32)[:, 0:SG]
        room = key_hot[:, :, :, :].rearrange("p a b c -> p (a b c)").bitcast(fp32)
        used = [0]

        def inside(n, rows=P):
            used[0] += n
            assert used[0] <= B0 * CH * KEYS // 2
            return room[0:rows, used[0] - n:used[0]]

        xs = x1
        dst_r = inside(SG, NS).bitcast(i32)
        diag = inside(7 * NS, NS).rearrange("p (a b) -> p a b", a=7)
        part_6, part_63, part_7 = (inside(NC).bitcast(i32) for _ in range(3))
        used[0] = 0
        messages = [inside(CH * D).rearrange("p (c d) -> p c d", c=CH) for _ in range(2)]
        dst_hot = [inside(CH * W1).rearrange("p (c w) -> p c w", c=CH) for _ in range(2)]
        ea_left = [inside(SG, RK) for _ in range(2)]
        ea_round = [counts_even[0:RK, :, :].rearrange("p a b -> p (a b)").bitcast(bf16)[:, n * SG:(n + 1) * SG] for n in range(2)]
        ea_mid = [counts_even[0:RK, :, :].rearrange("p a b -> p (a b)").bitcast(bf16)[:, n * SG:(n + 1) * SG] for n in range(2, 4)]
        ea_parts = [low_hot[0:RK, n, :, :].rearrange("p c e -> p (c e)") for n in range(2)]
        gathered = sb("gathered", [P, SLOTS, CH, D], fp32)
        ea_sb = sb("ea_sb", [RK, SLOTS, SG], fp32)
        hidden = sb("hidden", [DE, 2, SG], fp32)
        index = sb("index", [P, SLOTS, CH], i32)
        counts_odd = (gathered[:, :, :, :].rearrange("p a b c -> p (a b c)").bitcast(fp16)[:, 0:NT * B0 * VC]
                      .rearrange("p (a b) -> p a b", a=NT))
        counts = (counts_even, counts_odd)
        part_127 = gathered[:, :, :, :].rearrange("p a b c -> p (a b c)")[:, 0:NC].bitcast(i32)

        bank = [ctx.enter_context(nc.psum_tensor(f"bank{i}", [P, 512], fp32)) for i in range(8)]

        src_in, dst_in, nodes_in, weights_in = sem("src_in"), sem("dst_in"), sem("nodes_in"), sem("weights_in")
        late_const, bias_added = sem("late_const"), sem("bias_added")
        const_ready, ident_zero = sem("const_ready"), sem("ident_zero")
        v_step, sweep_step, fold_step = sem("v_step"), sem("sweep_step"), sem("fold_step")
        carrier = sem("carrier")
        xw_made, xw_taken = sem("xw_made"), sem("xw_taken")
        diag_ready, bases_spread, sweeps_ready = sem("diag_ready"), sem("bases_spread"), sem("sweeps_ready")
        hist_ready, hist_used, hist_done = sem("hist_ready"), sem("hist_used"), sem("hist_done")
        deg_ready, root_ready = sem("deg_ready"), sem("root_ready")
        inverse_ready, left_made, part_rounded, xs_ready = sem("inverse_ready"), sem("left_made"), sem("part_rounded"), sem("xs_ready")
        scal_ready, keys_ready, lows_away, lows_ready = (
            sem("scal_ready"), sem("keys_ready"), sem("lows_away"), sem("lows_ready"))
        counts_made = [sem(f"counts_made{i}") for i in range(4)]
        counts_taken = [sem(f"counts_taken{i}") for i in range(4)]
        sums_made, sums_taken, window_added = sem("sums_made"), sem("sums_taken"), sem("window_added")
        bases0_ready, bases0_used, bases1_ready = sem("bases0_ready"), sem("bases0_used"), sem("bases1_ready")
        layer0_done = sem("layer0_done")
        indeg_made, agg_made = sem("indeg_made"), sem("agg_made")
        var_ready, std_ready = sem("var_ready"), sem("std_ready")
        x1_ready, x1_stored, y_ready = sem("x1_ready"), sem("x1_stored"), sem("y_ready")
        turned, turn_taken, self_made, self_taken = sem("turned"), sem("turn_taken"), sem("self_made"), sem("self_taken")
        attrs_in = [sem(f"attrs_in{i}") for i in range(SLOTS)]
        index_in = [sem(f"index_in{i}") for i in range(SLOTS)]
        rows_in = [[sem(f"rows_in{i}_{h}") for h in range(2)] for i in range(SLOTS)]
        rounded, left_ready = sem("rounded"), sem("left_ready")
        mid_ready, parts_ready = sem("mid_ready"), sem("parts_ready")
        hidden_made, hidden_ready = sem("hidden_made"), sem("hidden_ready")
        weights_made, messages_ready = sem("weights_made"), sem("messages_ready")
        hot_ready, window_made, window_taken = sem("hot_ready"), sem("window_made"), sem("window_taken")
        layer1_done, sums1_made = sem("layer1_done"), sem("sums1_made")
        out_stored = sem("out_stored")

        def counter(engine, own):
            total = [0]

            def step():
                total[0] += 1
                return 1

            return step, lambda: engine.wait_ge(own, total[0])

        CONSTS, LATE = 9, 8
        rounds = NS // SLOTS
        per_slot = [rounds + (slot < NS % SLOTS) for slot in range(SLOTS)]
        assert NS % SLOTS == NS % B0 == NB % 2 == 1

        block = ctx.enter_context(nc.Block())

        @block.sync
        def _(sp):
            sp.dma_start(src_i[:, :], src_pm).then_inc(src_in, 16)
            sp.dma_start(dst_r, dst_rows).then_inc(dst_in, 16)
            sp.dma_start(dst_i[:, :], dst_pm).then_inc(dst_in, 16)
            sp.dma_start(x_sb[:, :, :], x_rows.rearrange("(t p) d -> p t d", p=P)).then_inc(nodes_in, 16)
            sp.dma_start(b0_sb[:, :], b0.broadcast_to([P, D])).then_inc(nodes_in, 16)
            for tile, source in ((w0_sb, w0e), (w1_rep, w1t), (masks, part_masks), (b1_sb, b1c), (w2_sb, w2e), (ws_sb, wse), (wn_sb, wnt), (xT, x_cols)):
                sp.dma_start(tile[:, :], source).then_inc(weights_in, 16)

            n_rows = x1_table.rearrange("(t p) d -> p t d", p=P)
            for g in range(TB):
                sp.wait_ge(x1_ready, g + 1)
                sp.dma_start(n_rows[:, g * BT:(g + 1) * BT, :], x1[:, g * BT:(g + 1) * BT, :]).then_inc(x1_stored, 16)

            n_sweeps = sp.value_load(sweeps_i[0:1, 1:2], min_val=1, max_val=SWEEPS1)

            def load(sweep, i, slot):
                n = sweep * NS + i
                sp.wait_ge(left_ready, n + 1)
                sp.dma_start(ea_sb[:, slot, :], ea_cols[:, bass.ds(i * SG, SG)]).then_inc(attrs_in[slot], 16)
                sp.wait_ge(messages_ready, n * 2 + 2)
                sp.dma_start(index[:, slot, :], src_pm[:, bass.ds(i * CH, CH)]).then_inc(index_in[slot], 16)

            with sp.Fori(0, n_sweeps) as sweep:
                sp.wait_ge(left_ready, sweep * NS + 4)
                sp.sem_inc(carrier, 1)
                sp.wait_ge(messages_ready, sweep * (NS * 2) + 8)
                sp.sem_inc(carrier, 1)
                with sp.Fori(0, rounds) as k:
                    for slot in range(SLOTS):
                        load(sweep, k * SLOTS + slot, slot)
                load(sweep, NS - 1, 0)

            for g in range(TB):
                rows = min((g + 1) * BT, NODES // P) - g * BT
                sp.wait_ge(y_ready, g + 1)
                sp.dma_start(out[g * BT * P:(g * BT + rows) * P, :].rearrange("(t p) d -> p t d", p=P),
                             y[:, g * BT:g * BT + rows, :]).then_inc(out_stored, 16)
            last = NODES // P
            sp.dma_start(out[last * P:NODES, :], y[0:NODES - last * P, last, :]).then_inc(out_stored, 16)
            sp.wait_ge(out_stored, (TB + 1) * 16)

        @block.gpsimd
        def _(pool):
            def numbers(tile, pattern):
                return pool.iota(tile, pattern, base=0, channel_multiplier=0, allow_small_or_imprecise_dtypes=True)

            numbers(iota_lo[:, :, :], [[1, LO], [0, CH]]).then_inc(const_ready, 1)
            pool.memset(zeros[:, :], 0.0).then_inc(const_ready, 1)
            pool.memset(ident[:, :], 0.0).then_inc(ident_zero, 1)
            pool.memset(ones[:, :], 1.0).then_inc(const_ready, 1)
            pool.wait_ge(ident_zero, 1)
            pool.affine_select(out=ident[:, :], in_=ident[:, :], compare_op=ALU.not_equal, fill=1.0, base=0,
                               pattern=[[-1, P]], channel_multiplier=1).then_inc(const_ready, 1)
            numbers(iota_sw[:, 0:SWEEPS0], [[W0, SWEEPS0]]).then_inc(const_ready, 1)
            numbers(iota_sw[:, SWEEPS0:], [[W1, SWEEPS1]]).then_inc(const_ready, 1)
            numbers(iota_key[:, :, :], [[1, NT], [NT, W0]]).then_inc(const_ready, 1)
            numbers(iota_row[:, :], [[1, P]]).then_inc(const_ready, 1)
            numbers(iota_neg[:, :], [[-1, P]]).then_inc(const_ready, 1)
            numbers(iota_w1[:, :], [[1, W1]]).then_inc(late_const, 1)
            pool.memset(xs_part[:, 0, :, D:DE], 1.0).then_inc(late_const, 1)
            pool.memset(xs_part[:, 1:3, :, D:DE], 0.0).then_inc(late_const, 1)
            pool.memset(agg0T[:, :], 0.0).then_inc(late_const, 1)
            pool.memset(agg1T[:, :], 0.0).then_inc(late_const, 1)
            pool.wait_ge(nodes_in, 32)
            pool.tensor_tensor(out=y[:, :, :], in0=x_sb[:, :, :], in1=b0_sb[:, :].unsqueeze(1).broadcast_to([P, NT, D]),
                               op=ALU.add).then_inc(bias_added, 1)
            pool.wait_ge(late_const, 5)
            pool.wait_ge(bias_added, 1)
            pool.memset(x1T[D:D + 2, :], 1.0).then_inc(late_const, 1)
            pool.memset(hidden[D:DE, :, :], 1.0).then_inc(late_const, 1)
            pool.wait_ge(late_const, 7)
            pool.sem_inc(late_const, 1)

            halves = (slice(0, NT // 2), slice(NT // 2, NT))
            pool.wait_ge(inverse_ready, 1)
            for h, tiles in enumerate(halves):
                pool.tensor_tensor(out=xs[:, tiles, :], in0=x_sb[:, tiles, :],
                                   in1=deg[:, 2, tiles].unsqueeze(2).broadcast_to([P, tiles.stop - tiles.start, D]),
                                   op=ALU.mult).then_inc(left_made, 1)
            for h, tiles in enumerate(halves):
                pool.wait_ge(part_rounded, h + 1)
                pool.tensor_tensor(out=xs[:, tiles, :], in0=xs[:, tiles, :], in1=xs_part[:, 0, tiles, 0:D],
                                   op=ALU.subtract).then_inc(left_made, 1)
            for h, tiles in enumerate(halves):
                pool.wait_ge(part_rounded, h + 3)
                pool.tensor_tensor(out=xs_part[:, 2, tiles, 0:D], in0=xs[:, tiles, :], in1=xs_part[:, 1, tiles, 0:D],
                                   op=ALU.subtract).then_inc(xs_ready, 1)

            pool.wait_ge(sweeps_ready, 1)
            n_sweeps = pool.value_load(sweeps_i[0:1, 0:1], min_val=1, max_val=SWEEPS0)
            pool.sem_inc(window_added, 1)
            pool.sem_inc(bases0_used, 1)

            def add_windows(sweep, b, supers):
                first_window = sweep * (NS * NG) + b * (B0 * NG)
                pool.wait_ge(sums_taken, sweep * (NB + 1) + b + 3)
                pool.sem_inc(carrier, 1)
                for some in range(0, supers * NG, 2 * NG):
                    these = range(some, min(some + 2 * NG, supers * NG))
                    bases = []
                    for g in these[::NG]:
                        bases += nc.values_load_multi_w_load_instructions(
                            base0_i[0:1, bass.ds(b * (B0 * NG) + g, NG)], [mybir.EngineType.Pool], min_val=0, max_val=NP,
                            skip_runtime_bounds_check_because="the bases are clamped on the chip")[1]
                    for g, base in zip(these, bases):
                        pool.wait_ge(window_added, first_window + g + 1)
                        pool.sem_inc(carrier, 1)
                        window = agg0T[:, bass.ds(base, W0)]
                        pool.tensor_tensor(out=window, in0=window, in1=window_sums[:, g * W0:(g + 1) * W0],
                                           op=ALU.add).then_inc(window_added, 1)

            with pool.Fori(0, n_sweeps) as sweep:
                pool.wait_ge(bases0_ready, sweep + 1)
                pool.sem_inc(carrier, 1)
                with pool.Fori(0, NB) as b:
                    add_windows(sweep, b, B0)
                add_windows(sweep, NB, NS - NB * B0)
                pool.sem_inc(bases0_used, 1)
            pool.wait_ge(window_added, n_sweeps * (NS * NG) + 1)
            pool.sem_inc(layer0_done, 1)

            n_sweeps = pool.value_load(sweeps_i[0:1, 1:2], min_val=1, max_val=SWEEPS1)
            pool.wait_ge(x1_stored, TB * 16)

            def gather(sweep, i, slot, nth):
                pool.wait_ge(messages_ready, (sweep * NS + i) * 2 + 2)
                pool.sem_inc(carrier, 1)
                pool.wait_ge(index_in[slot], (nth + 1) * 16)
                pool.sem_inc(carrier, 1)
                for c in range(CH):
                    pool.indirect_dma_start(out=gathered[:, slot, c, :], out_offset=None, in_=x1_table,
                                            in_offset=bass.IndirectOffsetOnAxis(ap=index[:, slot, c:c + 1], axis=0),
                                            ).then_inc(rows_in[slot][c * 2 // CH], 16)

            with pool.Fori(0, n_sweeps) as sweep:
                pool.wait_ge(messages_ready, sweep * (NS * 2) + 8)
                pool.sem_inc(carrier, 1)
                with pool.Fori(0, rounds) as k:
                    for slot in range(SLOTS):
                        gather(sweep, k * SLOTS + slot, slot, sweep * per_slot[slot] + k)
                gather(sweep, NS - 1, 0, sweep * per_slot[0] + rounds)

        @block.vector
        def _(ve):
            step, settle = counter(ve, v_step)

            ve.wait_ge(src_in, 16)
            for part, op, by in ((part_6, ALU.logical_shift_right, 6), (part_63, ALU.bitwise_and, LO - 1),
                                 (part_7, ALU.logical_shift_right, 7), (part_127, ALU.bitwise_and, P - 1)):
                ve.tensor_scalar(out=part, in0=src_i[:, :], scalar1=by, scalar2=None, op0=op).then_inc(v_step, step())
            settle()
            ve.tensor_copy(high6[:, :], part_6).then_inc(v_step, step())
            ve.tensor_copy(low6[:, :], part_63).then_inc(v_step, step())
            ve.tensor_scalar(out=key_low[:, :, 1], in0=part_127, scalar1=-1.0, scalar2=None,
                             op0=ALU.mult).then_inc(v_step, step())
            settle()
            ve.wait_ge(const_ready, CONSTS)

            def hist(s, slot):
                ve.wait_ge(hist_used, s + 1)
                for hot, width, part in ((lo_hot, LO, low6), (hi_hot, HI, high6)):
                    made = ve.tensor_tensor(
                        out=hot[:, slot, :, :], in0=iota_lo[:, 0:width, :],
                        in1=part[:, bass.ds(s * CH, CH)].unsqueeze(1).broadcast_to([P, width, CH]), op=ALU.is_equal)
                made.then_inc(hist_ready, 1)

            with ve.Fori(0, NS // 2) as k:
                hist(k * 2, 0)
                hist(k * 2 + 1, 1)
            hist(NS - 1, 0)

            def inverse_root(of, root, inv, tmp):
                ve.reciprocal(inv, root).then_inc(v_step, step())
                settle()
                ve.tensor_tensor(out=tmp, in0=inv, in1=inv, op=ALU.mult).then_inc(v_step, step())
                settle()
                ve.tensor_tensor(out=tmp, in0=tmp, in1=of, op=ALU.mult).then_inc(v_step, step())
                settle()
                ve.tensor_scalar(out=tmp, in0=tmp, scalar1=-0.5, scalar2=1.5, op0=ALU.mult, op1=ALU.add).then_inc(v_step, step())
                settle()
                ve.tensor_tensor(out=inv, in0=inv, in1=tmp, op=ALU.mult).then_inc(v_step, step())
                settle()

            ve.wait_ge(hist_done, 1)
            pairs = bank[1][0:LO, 0:HI].rearrange("p (t two) -> p t two", two=2)
            for half in range(2):
                ve.tensor_scalar(out=deg[half * LO:(half + 1) * LO, 0, :], in0=pairs[:, :, half], scalar1=1.0, scalar2=None,
                                 op0=ALU.max).then_inc(v_step, step())
            settle()
            ve.sem_inc(deg_ready, 1)

            ve.wait_ge(dst_in, 32)
            bases, ends, lengths = stats[:, 0:NG], stats[:, 8:8 + NG], stats[:, 12:12 + NG]
            base_all, widest, length_all, end_all = (stats[:, n:n + 1] for n in range(NG, NG + 4))
            ve.tensor_reduce(out=bases, in_=dst_r.rearrange("p (g e) -> p g e", g=NG), axis=AX.X, op=ALU.min).then_inc(v_step, step())
            ve.scalar_tensor_tensor(out=masked, in0=dst_r, scalar=float(NP), in1=dst_r, op0=ALU.is_lt,
                                    op1=ALU.mult).then_inc(v_step, step())
            ve.wait_ge(root_ready, 1)
            inverse_root(deg[:, 0, :], deg[:, 1, :], deg[:, 2, :], deg[:, 3, :])
            ve.sem_inc(inverse_ready, 1)
            ve.tensor_reduce(out=ends, in_=masked.rearrange("p (g e) -> p g e", g=NG), axis=AX.X, op=ALU.max).then_inc(v_step, step())
            ve.tensor_scalar(out=bases, in0=bases, scalar1=float(NP), scalar2=None, op0=ALU.min).then_inc(v_step, step())
            settle()
            ve.tensor_reduce(out=base_all, in_=bases, axis=AX.X, op=ALU.min).then_inc(v_step, step())
            ve.tensor_tensor(out=lengths, in0=ends, in1=bases, op=ALU.subtract).then_inc(v_step, step())
            ve.tensor_reduce(out=end_all, in_=ends, axis=AX.X, op=ALU.max).then_inc(v_step, step())
            settle()
            ve.tensor_reduce(out=widest, in_=lengths, axis=AX.X, op=ALU.max).then_inc(v_step, step())
            ve.tensor_tensor(out=length_all, in0=end_all, in1=base_all, op=ALU.subtract).then_inc(v_step, step())
            settle()
            for col in range(NG + 3):
                made = ve.tensor_scalar(out=diag[:, col, :], in0=ident[0:NS, 0:NS], scalar1=stats[:, col:col + 1],
                                        scalar2=None, op0=ALU.mult)
            made.then_inc(diag_ready, 1)
            ve.wait_ge(bases_spread, 1)
            spread = [bank[2 + col // 4][:, col % 4 * NS:(col % 4 + 1) * NS] for col in range(NG + 3)]
            dst_g = dst_i[:, :].rearrange("p (s g c) -> p s g c", g=NG, c=GC)
            key_g = key_low[:, :, 0].rearrange("p (s g c) -> p s g c", g=NG, c=GC)
            for g in range(NG):
                ve.tensor_tensor(out=key_g[:, :, g, :], in0=dst_g[:, :, g, :],
                                 in1=spread[g].unsqueeze(2).broadcast_to([P, NS, GC]),
                                 op=ALU.subtract).then_inc(v_step, step())
            ve.tensor_tensor(out=rel1[:, :].rearrange("p (s c) -> p s c", c=CH),
                             in0=dst_i[:, :].rearrange("p (s c) -> p s c", c=CH),
                             in1=spread[NG].unsqueeze(2).broadcast_to([P, NS, CH]),
                             op=ALU.subtract).then_inc(v_step, step())
            for g in range(NG):
                ve.tensor_copy(base0_f[:, :, g], spread[g][0:1, :]).then_inc(v_step, step())
            ve.tensor_copy(base1_f[:, :], spread[NG][0:1, :]).then_inc(v_step, step())
            for n in range(2):
                ve.tensor_reduce(out=spans[:, n:n + 1], in_=spread[NG + 1 + n][0:1, :], axis=AX.X,
                                 op=ALU.max).then_inc(v_step, step())
            settle()
            ve.scalar_tensor_tensor(out=key_low[:, :, 0], in0=key_low[:, :, 0], scalar=float(NT), in1=part_7,
                                    op0=ALU.mult, op1=ALU.add).then_inc(v_step, step())
            for n, (a, z) in enumerate(((0, SWEEPS0), (SWEEPS0, SWEEPS0 + SWEEPS1))):
                ve.tensor_scalar(out=within[:, a:z], in0=iota_sw[:, a:z], scalar1=spans[:, n:n + 1], scalar2=None,
                                 op0=ALU.is_le).then_inc(v_step, step())
            settle()
            for n, (a, z) in enumerate(((0, SWEEPS0), (SWEEPS0, SWEEPS0 + SWEEPS1))):
                ve.tensor_reduce(out=sweeps_f[:, n:n + 1], in_=within[:, a:z], axis=AX.X, op=ALU.add).then_inc(v_step, step())
            settle()
            ve.tensor_scalar(out=sweeps_i[:, :], in0=sweeps_f[:, :], scalar1=1.0, scalar2=None,
                             op0=ALU.max).then_inc(sweeps_ready, 1)

            ve.wait_ge(sweeps_ready, 1)
            n_sweeps = ve.value_load(sweeps_i[0:1, 0:1], min_val=1, max_val=SWEEPS0)

            def one_hots(sweep, s, q):
                n = sweep * NS + s
                ve.wait_ge(counts_taken[NG - 1], n + 1)
                ve.tensor_copy(scal[:, q, :, :], key_low[:, bass.ds(s * CH, CH), :]).then_inc(scal_ready, 1)
                ve.wait_ge(scal_ready, n + 1)
                for c in range(CH):
                    ve.tensor_scalar(out=key_hot[:, q, c, :], in0=iota_key[:, :, :].rearrange("p a b -> p (a b)"),
                                     scalar1=scal[:, q, c, 0:1], scalar2=None, op0=ALU.is_equal)
                ve.tensor_tensor(out=low_hot[:, q, 0:DVE_LOWS, :],
                                 in0=iota_neg[:, :].unsqueeze(1).broadcast_to([P, DVE_LOWS, P]),
                                 in1=scal[:, q, 0:DVE_LOWS, 1:2].broadcast_to([P, DVE_LOWS, P]),
                                 op=ALU.is_equal).then_inc(keys_ready, 1)

            with ve.Fori(0, n_sweeps) as sweep:
                ve.wait_ge(bases0_used, sweep + 1)
                ve.wait_ge(counts_taken[NG - 1], sweep * NS + B0)
                ve.tensor_scalar(out=base0_c[:, :], in0=base0_f[:, :, :].rearrange("p s g -> p (s g)"), scalar1=float(NP),
                                 scalar2=None, op0=ALU.min).then_inc(sweep_step, 1)
                ve.wait_ge(sweep_step, sweep * 3 + 1)
                ve.tensor_copy(base0_i[:, :], base0_c[:, :]).then_inc(bases0_ready, 1)
                with ve.Fori(0, NB) as b:
                    for q in range(B0):
                        one_hots(sweep, b * B0 + q, q)
                one_hots(sweep, NS - 1, 0)
                ve.wait_ge(keys_ready, (sweep + 1) * NS)
                ve.tensor_scalar(out=key_low[:, :, 0], in0=key_low[:, :, 0], scalar1=-float(KEYS), scalar2=None,
                                 op0=ALU.add).then_inc(sweep_step, 1)
                ve.tensor_scalar(out=base0_f[:, :, :], in0=base0_f[:, :, :], scalar1=float(W0), scalar2=None,
                                 op0=ALU.add).then_inc(sweep_step, 1)
                ve.wait_ge(sweep_step, sweep * 3 + 3)

            mean, half_gap, scatter, variance = (norms[:, n, :] for n in range(4))
            inverse, shift = deg[:, 2, :], norms[:, 4, :]

            def tiles_of(g):
                return slice(g * BT, (g + 1) * BT)

            def spread_tiles(column, tiles):
                return column[:, tiles].unsqueeze(2).broadcast_to([P, BT, D])

            def in_bank(b):
                return bank[b][:, 0:BT * D].rearrange("p (t d) -> p t d", t=BT)

            def tile_stats(source, g):
                for t in range(g * BT, (g + 1) * BT):
                    ve.bn_stats(out=bn6[:, t, :], in_=source[:, t, :]).then_inc(v_step, step())

            def norm(target, source, ready, nth):
                settle()
                ve.tensor_tensor(out=mean, in0=bn6[:, :, 1], in1=bn6[:, :, 4], op=ALU.add).then_inc(v_step, step())
                ve.tensor_tensor(out=half_gap, in0=bn6[:, :, 1], in1=bn6[:, :, 4], op=ALU.subtract).then_inc(v_step, step())
                ve.tensor_tensor(out=scatter, in0=bn6[:, :, 2], in1=bn6[:, :, 5], op=ALU.add).then_inc(v_step, step())
                settle()
                ve.tensor_scalar(out=mean, in0=mean, scalar1=0.5, scalar2=None, op0=ALU.mult).then_inc(v_step, step())
                ve.scalar_tensor_tensor(out=half_gap, in0=half_gap, scalar=0.25, in1=half_gap, op0=ALU.mult,
                                        op1=ALU.mult).then_inc(v_step, step())
                ve.tensor_scalar(out=scatter, in0=scatter, scalar1=1.0 / D, scalar2=EPS, op0=ALU.mult,
                                 op1=ALU.add).then_inc(v_step, step())
                settle()
                ve.tensor_tensor(out=variance, in0=scatter, in1=half_gap, op=ALU.add).then_inc(v_step, step())
                settle()
                ve.sem_inc(var_ready, 1)
                ve.wait_ge(std_ready, nth)
                inverse_root(variance, deg[:, 1, :], inverse, deg[:, 3, :])
                for g in range(TB):
                    for t in range(g * BT, (g + 1) * BT):
                        ve.tensor_scalar(out=target[:, t, :], in0=source[:, t, :], scalar1=mean[:, t:t + 1],
                                         scalar2=inverse[:, t:t + 1], op0=ALU.subtract,
                                         op1=ALU.mult).then_inc(ready if t % BT == BT - 1 else v_step,
                                                                1 if t % BT == BT - 1 else step())

            ve.wait_ge(indeg_made, 1)
            in_degree = bank[0][:, 0:NT]
            ve.tensor_scalar(out=deg[:, 0, :], in0=in_degree, scalar1=1.0, scalar2=None, op0=ALU.max).then_inc(v_step, step())
            ve.tensor_scalar(out=deg[:, 4, :], in0=in_degree, scalar1=0.0, scalar2=None, op0=ALU.is_equal).then_inc(v_step, step())
            settle()
            ve.sem_inc(deg_ready, 1)
            ve.wait_ge(xw_taken, TB)
            ve.wait_ge(bias_added, 1)
            for t in range(NT):
                ve.scalar_tensor_tensor(out=xw[:, t, :], in0=xw[:, t, :], scalar=deg[:, 4, t:t + 1], in1=y[:, t, :],
                                        op0=ALU.mult, op1=ALU.add).then_inc(v_step, step())
            ve.wait_ge(root_ready, 2)
            inverse_root(deg[:, 0, :], deg[:, 1, :], inverse, deg[:, 3, :])
            for g in range(TB):
                ve.wait_ge(agg_made, g + 1)
                ve.tensor_tensor(out=x1[:, tiles_of(g), :], in0=in_bank(1 + g), in1=spread_tiles(inverse, tiles_of(g)),
                                 op=ALU.mult).then_inc(v_step, step())
            settle()
            for g in range(TB):
                ve.tensor_tensor(out=xw[:, tiles_of(g), :], in0=xw[:, tiles_of(g), :], in1=x1[:, tiles_of(g), :],
                                 op=ALU.add).then_inc(v_step, step())
            settle()
            for g in range(TB):
                tile_stats(xw, g)
            norm(x1, xw, x1_ready, 1)

            n_sweeps = ve.value_load(sweeps_i[0:1, 1:2], min_val=1, max_val=SWEEPS1)
            ve.sem_inc(messages_ready, 8)
            ve.sem_inc(window_taken, 2)
            ve.sem_inc(left_ready, 4)
            ve.sem_inc(parts_ready, 1)
            ve.wait_ge(weights_in, 8 * 16)
            piece = [messages[0][0:RK, n, :] for n in range(3)]
            for n in range(3):
                ve.tensor_copy(w1_sb[:, 0, :], w1_rep[:, :]).then_inc(v_step, step())
                settle()
                ve.tensor_copy(piece[n], w1_sb[:, 0, :]).then_inc(v_step, step())
                ve.tensor_tensor(out=w1_rep[:, :], in0=w1_rep[:, :], in1=w1_sb[:, 0, :],
                                 op=ALU.subtract).then_inc(v_step, step())
                settle()
            for half in range(2):
                for n in range(3):
                    ve.scalar_tensor_tensor(out=w1_sb[:, half, :], in0=piece[n], scalar=masks[:, 2 + 3 * half + n:3 + 3 * half + n],
                                            in1=w1_rep[:, :] if n == 0 else w1_sb[:, half, :],
                                            op0=ALU.mult, op1=ALU.add).then_inc(v_step, step())
                    settle()

            def less_first(n, slot, place):
                ve.wait_ge(rounded, n + 1)
                ve.wait_ge(parts_ready, n + 1)
                ve.scalar_tensor_tensor(out=ea_left[place], in0=ea_round[place], scalar=masks[:, 0:1], in1=ea_sb[:, slot, :],
                                        op0=ALU.mult, op1=ALU.add).then_inc(left_ready, 1)

            def split(n, place):
                ve.wait_ge(mid_ready, n + 1)
                ve.scalar_tensor_tensor(out=ea_parts[place], in0=ea_mid[place], scalar=masks[:, 1:2], in1=ea_left[place],
                                        op0=ALU.mult, op1=ALU.add).then_inc(parts_ready, 1)

            def fold(sweep, i, slot, nth, i_next):
                n = sweep * NS + i
                if i_next:
                    less_first(n + 2, (slot + 2) % SLOTS, slot % 2)
                base = ve.value_load(base1_i[0:1, bass.ds(i, 1)], min_val=0, max_val=NP)
                ve.wait_ge(window_made, n + 1)
                ve.tensor_tensor(out=dst_hot[slot % 2], in0=iota_w1[:, :].unsqueeze(1).broadcast_to([P, CH, W1]),
                                 in1=rel1[:, bass.ds(i * CH, CH)].unsqueeze(2).broadcast_to([P, CH, W1]),
                                 op=ALU.is_equal).then_inc(hot_ready, 1)
                for h in range(2):
                    ve.wait_ge(rows_in[slot][h], (nth + 1) * (CH // 2 * 16))
                    ve.wait_ge(weights_made, n * 2 + h + 5)
                    half = slice(h * CH // 2, (h + 1) * CH // 2)
                    ve.tensor_tensor(out=messages[slot % 2][:, half, :],
                                     in0=bank[2 + 2 * (slot % 2) + h][:, 0:CH // 2 * D].rearrange("p (c d) -> p c d", d=D),
                                     in1=gathered[:, slot, half, :], op=ALU.mult).then_inc(messages_ready, 1)
                if i_next:
                    split(n + 2, slot % 2)
                ve.wait_ge(window_made, n + 3)
                ve.wait_ge(window_taken, n + 2)
                window = agg1T[0:D, bass.ds(base, W1)]
                ve.tensor_tensor(out=window, in0=window, in1=bank[6 + slot % 2][0:D, 0:W1], op=ALU.add).then_inc(window_taken, 1)

            with ve.Fori(0, n_sweeps) as sweep:
                ve.wait_ge(window_made, sweep * NS + 2)
                ve.tensor_scalar(out=base1_c[:, :], in0=base1_f[:, :], scalar1=float(NP), scalar2=None,
                                 op0=ALU.min).then_inc(fold_step, 1)
                ve.wait_ge(fold_step, sweep * 4 + 1)
                ve.tensor_copy(base1_i[:, :], base1_c[:, :]).then_inc(fold_step, 1)
                ve.wait_ge(fold_step, sweep * 4 + 2)
                ve.sem_inc(carrier, 1)
                for first in range(2):
                    less_first(sweep * NS + first, first, first)
                    split(sweep * NS + first, first)
                with ve.Fori(0, rounds - 1) as k:
                    for slot in range(SLOTS):
                        fold(sweep, k * SLOTS + slot, slot, sweep * per_slot[slot] + k, True)
                for i in range(NS - 1 - SLOTS, NS):
                    fold(sweep, i, i % SLOTS, sweep * per_slot[i % SLOTS] + i // SLOTS, i + 2 < NS)
                ve.wait_ge(hot_ready, (sweep + 1) * NS)
                ve.tensor_scalar(out=rel1[:, :], in0=rel1[:, :], scalar1=-float(W1), scalar2=None,
                                 op0=ALU.add).then_inc(fold_step, 1)
                ve.tensor_scalar(out=base1_f[:, :], in0=base1_f[:, :], scalar1=float(W1), scalar2=None,
                                 op0=ALU.add).then_inc(fold_step, 1)
                ve.wait_ge(fold_step, sweep * 4 + 4)
            ve.wait_ge(window_taken, n_sweeps * NS + 2)
            ve.sem_inc(layer1_done, 1)

            ve.wait_ge(self_taken, TB)
            for g in range(TB):
                ve.wait_ge(sums1_made, g + 1)
                ve.tensor_tensor(out=xw[:, tiles_of(g), :], in0=xw[:, tiles_of(g), :], in1=in_bank(g),
                                 op=ALU.add).then_inc(v_step, step())
            settle()
            for g in range(TB):
                ve.scalar_tensor_tensor(out=xw[:, tiles_of(g), :], in0=xw[:, tiles_of(g), :], scalar=0.0,
                                        in1=x1[:, tiles_of(g), :], op0=ALU.max, op1=ALU.add).then_inc(v_step, step())
            settle()
            for g in range(TB):
                tile_stats(xw, g)
            norm(y, xw, y_ready, 2)

        @block.scalar
        def _(ac):
            def to_xw(g, b, done):
                ac.activation(xw[:, g * BT:(g + 1) * BT, :], bank[b][:, 0:BT * D].rearrange("p (t d) -> p t d", t=BT),
                              ACT.Copy).then_inc(done, 1)

            for taken in counts_taken:
                ac.sem_inc(taken, B0)
            ac.sem_inc(sums_taken, 2)
            ac.wait_ge(deg_ready, 1)
            ac.activation(deg[:, 1, :], deg[:, 0, :], ACT.Sqrt).then_inc(root_ready, 1)

            def round_part(part):
                for h, tiles in enumerate((slice(0, NT // 2), slice(NT // 2, NT))):
                    ac.wait_ge(left_made, part * 2 + h + 1)
                    ac.activation(xs_part[:, part, tiles, 0:D], xs[:, tiles, :], ACT.Copy).then_inc(part_rounded, 1)

            round_part(0)
            for g in range(TB):
                ac.wait_ge(xw_made, g + 1)
                to_xw(g, (0, 4, 5, 6, 7)[g], xw_taken)
            round_part(1)

            ac.wait_ge(sweeps_ready, 1)
            n_sweeps = ac.value_load(sweeps_i[0:1, 0:1], min_val=1, max_val=SWEEPS0)

            def lows(sweep, s, q):
                n = sweep * NS + s
                ac.wait_ge(scal_ready, n + 1)
                ac.wait_ge(lows_ready, n + 1)
                for c in range(DVE_LOWS, CH):
                    ac.activation(away[:, c - DVE_LOWS, :], iota_row[:, :], ACT.Abs,
                                  bias=scal[:, q, c, 1:2]).then_inc(lows_away, 1)
                ac.wait_ge(lows_away, (n + 1) * (CH - DVE_LOWS))
                ac.activation(low_hot[:, q, DVE_LOWS:CH, :], away[:, :, :], ACT.Relu, bias=1.0,
                              scale=-1.0).then_inc(lows_ready, 1)

            def take_counts(sweep, b, parity, q):
                for g in range(NG):
                    ac.wait_ge(counts_made[g], sweep * NS + b * B0 + q + 1)
                    ac.activation(counts[parity][:, :, q * VC + g * W0:q * VC + (g + 1) * W0],
                                  bank[g][:, 0:KEYS].rearrange("p (a b) -> p a b", a=NT), ACT.Copy).then_inc(counts_taken[g], 1)

            def take_sums(sweep, b, parity, supers):
                ac.wait_ge(sums_made, sweep * (NB + 1) + b + 1)
                ac.wait_ge(window_added, sweep * (NS * NG) + b * (B0 * NG) + 1)
                ac.activation(window_sums[:, 0:supers * VC], bank[4 + parity][0:DE, 0:supers * VC],
                              ACT.Copy).then_inc(sums_taken, 1)

            def batch(sweep, b, parity, last=B0):
                for q in range(B0):
                    take_counts(sweep, b, parity, q)
                    if q < last:
                        lows(sweep, b * B0 + q + B0 - 1, (q + B0 - 1) % B0)

            ac.sem_inc(lows_ready, 1)
            with ac.Fori(0, n_sweeps) as sweep:
                for q in range(B0 - 1):
                    lows(sweep, q, q)
                batch(sweep, 0, 0)
                with ac.Fori(0, NB // 2 - 1) as k:
                    for b, parity in ((k * 2 + 1, 1), (k * 2 + 2, 0)):
                        batch(sweep, b, parity)
                        take_sums(sweep, b - 1, 1 - parity, B0)
                for b in (NB - 2, NB - 1):
                    batch(sweep, b, b % 2, last=min(B0, NS - B0 + 1 - b * B0))
                    take_sums(sweep, b - 1, 1 - b % 2, B0)
                take_counts(sweep, NB, NB % 2, 0)
                take_sums(sweep, NB - 1, 1 - NB % 2, B0)
                take_sums(sweep, NB, NB % 2, NS - NB * B0)

            ac.wait_ge(deg_ready, 2)
            ac.activation(deg[:, 1, :], deg[:, 0, :], ACT.Sqrt).then_inc(root_ready, 1)
            ac.wait_ge(var_ready, 1)
            ac.activation(deg[:, 1, :], norms[:, 3, :], ACT.Sqrt).then_inc(std_ready, 1)

            for k in range(-(-NT // 4)):
                tiles = min(4, NT - k * 4)
                ac.wait_ge(turned, k + 1)
                ac.activation(x1T[0:D, k * 4 * P:(k * 4 + tiles) * P], bank[k][0:D, 0:tiles * P], ACT.Copy).then_inc(turn_taken, 1)

            for g in range(TB):
                ac.wait_ge(self_made, g + 1)
                to_xw(g, (7, 0, 1, 2, 3)[g], self_taken)

            n_sweeps = ac.value_load(sweeps_i[0:1, 1:2], min_val=1, max_val=SWEEPS1)
            ac.sem_inc(hidden_ready, 8)

            def rectify(sweep, i, slot):
                n = sweep * NS + i
                ac.wait_ge(weights_made, n * 2 + 2)
                for h in range(2):
                    ac.wait_ge(hidden_made, n * 2 + h + 1)
                    ac.activation(hidden[0:D, slot, h * 512:(h + 1) * 512], bank[h][0:D, :], ACT.Relu,
                                  bias=b1_sb[:, 0:1]).then_inc(hidden_ready, 1)

            def round_first(n, slot, nth, place):
                ac.wait_ge(attrs_in[slot], (nth + 1) * 16)
                ac.activation(ea_round[place], ea_sb[:, slot, :], ACT.Copy).then_inc(rounded, 1)

            def round_second(n, place):
                ac.wait_ge(left_ready, n + 5)
                ac.activation(ea_mid[place], ea_left[place], ACT.Copy).then_inc(mid_ready, 1)

            def rounds_of(sweep, i, ahead):
                return sweep * per_slot[(i + ahead) % SLOTS]

            with ac.Fori(0, n_sweeps) as sweep:
                ac.wait_ge(weights_made, sweep * (NS * 2) + 4)
                ac.sem_inc(carrier, 1)
                for i in range(2):
                    round_first(sweep * NS + i, i, rounds_of(sweep, i, 0), i)
                for i in range(2):
                    round_second(sweep * NS + i, i)
                round_first(sweep * NS + 2, 2, rounds_of(sweep, 2, 0), 0)
                rectify(sweep, 0, 0)
                with ac.Fori(0, rounds - 1) as k:
                    for slot in range(SLOTS):
                        i = k * SLOTS + slot
                        round_second(sweep * NS + i + 2, slot % 2)
                        rectify(sweep, i + 1, (slot + 1) % 2)
                        round_first(sweep * NS + i + 3, (slot + 3) % SLOTS,
                                    rounds_of(sweep, slot, 3) + k + (slot + 3) // SLOTS, (slot + 1) % 2)
                for i in range(NS - 1 - SLOTS, NS - 1):
                    if i + 2 < NS:
                        round_second(sweep * NS + i + 2, i % 2)
                    rectify(sweep, i + 1, (i + 1) % 2)
                    if i + 3 < NS:
                        round_first(sweep * NS + i + 3, (i + 3) % SLOTS, rounds_of(sweep, i, 3) + (i + 3) // SLOTS, (i + 1) % 2)
            ac.wait_ge(var_ready, 2)
            ac.activation(deg[:, 1, :], norms[:, 3, :], ACT.Sqrt).then_inc(std_ready, 1)

        @block.tensor
        def _(te):
            te.wait_ge(const_ready, CONSTS)

            te.sem_inc(hist_used, 2)
            tally = bank[1][0:LO, 0:HI]
            te.matmul(tally, zeros[:, 0:LO], zeros[:, 0:HI], start=True, stop=False)

            def hist(s, slot):
                te.wait_ge(hist_ready, s + 1)
                for c in range(CH):
                    made = te.matmul(tally, lo_hot[:, slot, :, c], hi_hot[:, slot, :, c], start=False, stop=False)
                made.then_inc(hist_used, 1)

            with te.Fori(0, NS // 2) as k:
                hist(k * 2, 0)
                hist(k * 2 + 1, 1)
            hist(NS - 1, 0)
            te.matmul(tally, zeros[:, 0:LO], zeros[:, 0:HI], start=False, stop=True).then_inc(hist_done, 1)

            def project(first, last):
                for g in range(first, last):
                    for t in range(BT):
                        at = (g * BT + t) * P
                        made = te.matmul(bank[(0, 4, 5, 6, 7)[g]][:, t * D:(t + 1) * D], xT[:, at:at + P], w0_sb[0:D, 0:D],
                                         start=True, stop=True)
                    made.then_inc(xw_made, 1)

            te.wait_ge(weights_in, 8 * 16)
            project(0, 3)
            te.wait_ge(diag_ready, 1)
            for a, z in ((0, 4), (4, NG + 3)):
                made = te.matmul(bank[2 + a // 4][:, 0:(z - a) * NS], ones[0:NS, :], diag[:, a:z, :].rearrange("p a b -> p (a b)"),
                                 start=True, stop=True)
            made.then_inc(bases_spread, 1)
            project(3, TB)

            te.wait_ge(sweeps_ready, 1)
            n_sweeps = te.value_load(sweeps_i[0:1, 0:1], min_val=1, max_val=SWEEPS0)
            te.wait_ge(xw_taken, TB)

            def count(sweep, b, q):
                n = sweep * NS + b * B0 + q
                te.wait_ge(keys_ready, n + 1)
                te.wait_ge(lows_ready, n + 2)
                for g in range(NG):
                    te.wait_ge(counts_taken[g], n + B0)
                    for c in range(g * GC, (g + 1) * GC):
                        made = te.matmul(bank[g][:, 0:KEYS], low_hot[:, q, c, :], key_hot[:, q, c, :],
                                         start=c == g * GC, stop=c == (g + 1) * GC - 1)
                    made.then_inc(counts_made[g], 1)

            def sums(sweep, b, parity, supers, quarter):
                if quarter == 0:
                    for g in range(NG):
                        te.wait_ge(counts_taken[g], sweep * NS + b * B0 + supers + B0)
                    te.wait_ge(sums_taken, sweep * (NB + 1) + b + 1)
                for a in range(quarter * NT // 4, (quarter + 1) * NT // 4):
                    for part in range(3):
                        made = te.matmul(bank[4 + parity][0:DE, 0:supers * VC], xs_part[:, part, a, :],
                                         counts[parity][:, a, 0:supers * VC],
                                         start=a == part == 0, stop=a == NT - 1 and part == 2)
                if quarter == 3:
                    made.then_inc(sums_made, 1)

            with te.Fori(0, n_sweeps) as sweep:
                for q in range(B0):
                    count(sweep, 0, q)
                te.wait_ge(xs_ready, 2)
                with te.Fori(0, NB // 2) as k:
                    for b, parity in ((k * 2 + 1, 1), (k * 2 + 2, 0)):
                        for q in range(B0):
                            count(sweep, b, q)
                            sums(sweep, b - 1, 1 - parity, B0, q)
                count(sweep, NB, 0)
                for quarter in range(4):
                    sums(sweep, NB - 1, 1 - NB % 2, B0, quarter)
                for quarter in range(4):
                    sums(sweep, NB, NB % 2, NS - NB * B0, quarter)

            te.wait_ge(layer0_done, 1)
            for t in range(NT):
                made = te.matmul(bank[0][:, t:t + 1], agg0T[:, t * P:(t + 1) * P], w0_sb[:, D:DE], start=True, stop=True)
            made.then_inc(indeg_made, 1)
            for g in range(TB):
                for t in range(BT):
                    at = (g * BT + t) * P
                    made = te.matmul(bank[1 + g][:, t * D:(t + 1) * D], agg0T[0:D, at:at + P], w0_sb[0:D, 0:D], start=True, stop=True)
                made.then_inc(agg_made, 1)

            for k in range(-(-NT // 4)):
                tiles = min(4, NT - k * 4)
                te.wait_ge(x1_ready, (k * 4 + tiles - 1) // BT + 1)
                for t in range(tiles):
                    made = te.transpose(bank[k][0:D, t * P:(t + 1) * P], x1[:, k * 4 + t, :], ident[:, :])
                made.then_inc(turned, 1)

            te.wait_ge(late_const, LATE)
            for g in range(TB):
                te.wait_ge(turn_taken, min(-(-NT // 4), (g + 1) * BT // 4 + 1))
                for t in range(BT):
                    at = (g * BT + t) * P
                    made = te.matmul(bank[(7, 0, 1, 2, 3)[g]][:, t * D:(t + 1) * D], x1T[:, at:at + P], ws_sb[:, :],
                                     start=True, stop=True)
                made.then_inc(self_made, 1)

            n_sweeps = te.value_load(sweeps_i[0:1, 1:2], min_val=1, max_val=SWEEPS1)
            te.sem_inc(weights_made, 4)
            te.sem_inc(window_made, 2)
            te.wait_ge(self_taken, TB)

            def hide(n, place, h):
                te.wait_ge(parts_ready, n + 2)
                te.wait_ge(hidden_ready, n * 2 + h + 7)
                te.matmul(bank[h][0:D, :], w1_sb[:, 0, :], ea_parts[place][:, h * 512:(h + 1) * 512], start=True, stop=False)
                te.matmul(bank[h][0:D, :], w1_sb[:, 1, :], ea_parts[place][:, h * 512:(h + 1) * 512], start=False,
                          stop=True).then_inc(hidden_made, 1)

            def weigh(n, slot, h):
                te.wait_ge(hidden_ready, n * 2 + h + 9)
                te.wait_ge(messages_ready, n * 2 + h + 5)
                for c in range(CH // 2):
                    at = h * 512 + c * P
                    made = te.matmul(bank[2 + 2 * (slot % 2) + h][:, c * D:(c + 1) * D], hidden[:, slot % 2, at:at + P],
                                     w2_sb[:, :], start=True, stop=True)
                made.then_inc(weights_made, 1)

            def gather_sums(n, slot, h):
                if h == 0:
                    te.wait_ge(hot_ready, n + 1)
                    te.wait_ge(window_taken, n + 1)
                te.wait_ge(messages_ready, n * 2 + h + 9)
                for c in range(h * CH // 2, (h + 1) * CH // 2):
                    made = te.matmul(bank[6 + slot % 2][0:D, 0:W1], messages[slot % 2][:, c, :], dst_hot[slot % 2][:, c, :],
                                     start=c == 0, stop=c == CH - 1)
                if h == 1:
                    made.then_inc(window_made, 1)

            with te.Fori(0, n_sweeps) as sweep:
                te.wait_ge(messages_ready, sweep * (NS * 2) + 8)
                te.wait_ge(window_taken, sweep * NS + 2)
                te.sem_inc(carrier, 1)
                for h in range(2):
                    hide(sweep * NS, 0, h)
                for h in range(2):
                    weigh(sweep * NS, 0, h)
                with te.Fori(0, rounds) as k:
                    for slot in range(SLOTS):
                        n = sweep * NS + k * SLOTS + slot
                        after = (slot + 1) % SLOTS
                        for h in range(2):
                            hide(n + 1, after % 2, h)
                            gather_sums(n, slot, h)
                            weigh(n + 1, after, h)
                for h in range(2):
                    gather_sums(sweep * NS + NS - 1, 0, h)

            te.wait_ge(layer1_done, 1)
            for g in range(TB):
                for t in range(BT):
                    at = (g * BT + t) * P
                    made = te.matmul(bank[g][:, t * D:(t + 1) * D], agg1T[:, at:at + P], wn_sb[:, :], start=True, stop=True)
                made.then_inc(sums1_made, 1)


def kernel(x, src, dst, edge_attr_17, L0_gnn_weight, L0_gnn_bias, L1_gnn_W1, L1_gnn_b1, L1_gnn_W2, L1_gnn_b2,
           L1_gnn_Ws, L1_gnn_bs, L1_gnn_Wn, L1_gnn_bn):
    import numpy as np
    import concourse.bacc as bacc
    from concourse.bass_utils import run_bass_kernel_spmd

    def padded(a, shape, fill=0):
        a = np.asarray(a)
        whole = np.full(shape, fill, a.dtype)
        whole[tuple(slice(0, n) for n in a.shape)] = a
        return whole

    x = np.asarray(x)
    src_pad, dst_pad = padded(src, (NC * P,), PAD_SRC), padded(dst, (NC * P,), PAD_DST)
    weight = padded(L0_gnn_weight, (DE, DE))
    weight[D, D] = 1
    x_pad = padded(x, (NP, D))

    def with_bias(w, b):
        return np.concatenate([np.asarray(w).T, np.asarray(b)[None]])

    rows = np.repeat(np.arange(len(ROW_PARTS)), ED)
    part_masks = np.stack([-1.0 * (np.array(ROW_PARTS)[rows] > n) for n in (1, 2)]
                          + [np.array(parts)[rows] == n for parts in W_PARTS for n in (1, 2, 3)], 1).astype(np.float32)

    arrays = {
        "x_rows": x_pad,
        "x_cols": x_pad.T,
        "src_pm": src_pad.reshape(NC, P).T,
        "dst_pm": dst_pad.reshape(NC, P).T,
        "dst_rows": dst_pad.reshape(NS, SG),
        "ea_cols": np.tile(padded(edge_attr_17, (NC * P, ED)).T, (len(ROW_PARTS), 1)),
        "w0e": weight,
        "b0": np.asarray(L0_gnn_bias)[None],
        "w1t": np.tile(np.asarray(L1_gnn_W1).T, (len(ROW_PARTS), 1)),
        "b1c": np.asarray(L1_gnn_b1)[:, None],
        "w2e": with_bias(L1_gnn_W2, L1_gnn_b2),
        "wse": np.concatenate([with_bias(L1_gnn_Ws, L1_gnn_bs), np.asarray(L1_gnn_bn)[None]]),
        "wnt": np.asarray(L1_gnn_Wn).T,
        "part_masks": part_masks,
    }
    arrays = {name: np.ascontiguousarray(a) for name, a in arrays.items()}
    nc = bacc.Bacc("TRN2", target_bir_lowering=False, num_devices=1)
    args = [nc.dram_tensor(name, a.shape, mybir.dt.from_np(a.dtype), kind="ExternalInput").ap() for name, a in arrays.items()]
    out = nc.dram_tensor("out", (NODES, D), mybir.dt.float32, kind="ExternalOutput").ap()
    build(nc, *args, out)
    return run_bass_kernel_spmd(nc, [arrays], core_ids=[0]).results[0]["out"]
```

```python
from contextlib import ExitStack

import concourse.bass as bass
from concourse import mybir

NODES, D, EDGES, ED = 3125, 96, 103125, 17
P = 128
NT = -(-NODES // P)
NP = NT * P
DE = D + 1
CH = 8
SG = CH * P
NS = -(-EDGES // SG)
NC = NS * CH
NG = 4
GC = CH // NG
W0, W1 = 11, 48
KEYS = W0 * NT
B0 = 4
NB = NS // B0
VC = NG * W0
IC = 4
LO = 64
HI = NP // LO
HC = 2 * CH
HISTS, HIST_UNROLL = NC // HC, 4
PAD_DST, PAD_SRC = 4095, NP - 1
SLOTS = 4
DENSE = CH - 1
MIDDLE = NP // 2
SWEEPS0, SWEEPS1 = -(-NP // W0) + 1, -(-NP // W1) + 1
BT = 5
TB = NT // BT
DVE_GROUPS = 3
EPS = 1e-5
ROW_PARTS = (1, 1, 1, 2, 2, 3, 3)
W_PARTS = ((1, 2, 3, 1, 2, 1, 2), (0, 0, 0, 3, 0, 3, 0))
RK = ED * len(ROW_PARTS)


def build(nc, x_rows, x_cols, src_pm, src_rows, dst_pm, dst_rows, ea_cols, w0e, b0, w1t, b1c, w2e, wse, wnt, part_masks, out):
    fp32, bf16, fp16, i32 = mybir.dt.float32, mybir.dt.bfloat16, mybir.dt.float16, mybir.dt.int32
    ALU, ACT, AX = mybir.AluOpType, mybir.ActivationFunctionType, mybir.AxisListType

    src_near = nc.dram_tensor("src_near", (NS, P), fp16, kind="Internal").ap()
    x1_table = nc.dram_tensor("x1_table", (NP, D), fp32, kind="Internal").ap()

    with ExitStack() as ctx:
        def sb(name, shape, dt):
            return ctx.enter_context(nc.sbuf_tensor(name, shape, dt))

        def sem(name):
            return ctx.enter_context(nc.semaphore(name))

        src_i = sb("src_i", [P, NC], i32)
        dst_i = sb("dst_i", [P, NC], i32)
        x_sb = sb("x_sb", [P, NT, D], fp32)
        w0_sb = sb("w0_sb", [DE, DE], fp32)
        b0_sb = sb("b0_sb", [P, D], fp32)
        w1_rep = sb("w1_rep", [RK, D], fp32)
        w1_sb = sb("w1_sb", [RK, 2, D], bf16)
        masks = sb("masks", [RK, 8], fp32)
        b1_sb = sb("b1_sb", [D, 1], fp32)
        w2_sb = sb("w2_sb", [DE, D], fp32)
        ws_sb = sb("ws_sb", [D + 2, D], fp32)
        wn_sb = sb("wn_sb", [D, D], fp32)
        iota_key = sb("iota_key", [P, NT, W0, IC], fp16)
        iota_low = sb("iota_low", [P, P, IC], fp16)
        iota_w1 = sb("iota_w1", [P, W1], fp32)
        iota_sw = sb("iota_sw", [1, SWEEPS0 + SWEEPS1], fp32)
        ident = sb("ident", [P, P], fp32)
        ones = sb("ones", [P, P], fp32)
        zeros = sb("zeros", [P, LO], bf16)
        low6 = sb("low6", [P, NC], fp16)
        high6 = sb("high6", [P, NC], fp16)
        key = sb("key", [P, NC], fp32)
        key_near = sb("key_near", [P, NC], fp16)
        low7 = sb("low7", [P, NC], fp16)
        rel1 = sb("rel1", [P, NC], fp32)
        stats = sb("stats", [NS, 16], fp32)
        base0_f = sb("base0_f", [1, NS, NG], fp32)
        base1_f = sb("base1_f", [1, NS], fp32)
        base0_c = sb("base0_c", [1, NS * NG], fp32)
        base1_c = sb("base1_c", [1, NS], fp32)
        base0_i = sb("base0_i", [1, NS * NG], i32)
        base1_i = sb("base1_i", [1, NS], i32)
        spans = sb("spans", [1, 2], fp32)
        within = sb("within", [1, SWEEPS0 + SWEEPS1], fp32)
        sweeps_f = sb("sweeps_f", [1, 2], fp32)
        sweeps_i = sb("sweeps_i", [1, 2], i32)
        deg = sb("deg", [P, 6, NT], fp32)
        xs_part = sb("xs_part", [P, 3, NT, DE], bf16)
        xw = sb("xw", [P, NT, D], fp32)
        agg0T = sb("agg0T", [DE, NP + W0], fp32)
        x1 = sb("x1", [P, NT, D], fp32)
        bn6 = sb("bn6", [P, NT, 6], fp32)
        norms = sb("norms", [P, 6, NT], fp32)
        y = sb("y", [P, NT, D], fp32)
        x1T = sb("x1T", [D + 2, NP], fp32)
        xT = x1T[0:D, :]
        agg1T = sb("agg1T", [D, NP + W1], fp32)
        low_hot = sb("low_hot", [P, B0, CH // IC, P, IC], bf16)
        key_hot = sb("key_hot", [P, B0, CH // IC, KEYS, IC], bf16)
        counts_even = sb("counts", [P, NT, B0 * VC], fp16)
        window_sums = sb("window_sums", [DE, B0 * VC], fp32)
        masked = counts_even[0:NS, :, :].rearrange("p a b -> p (a b)").bitcast(fp32)[:, 0:SG]
        room = key_hot[:, :, :, :, :].rearrange("p a b c d -> p (a b c d)").bitcast(fp32)
        used = [0]

        def inside(n, rows=P):
            used[0] += n
            assert used[0] <= B0 * CH * KEYS // 2
            return room[0:rows, used[0] - n:used[0]]

        xs = x1
        dst_r = inside(SG, NS).bitcast(i32)
        diag = inside(7 * NS, NS).rearrange("p (a b) -> p a b", a=7)
        part_6, part_63, part_7 = (inside(NC).bitcast(i32) for _ in range(3))
        used[0] = 0
        messages = [inside(CH * D).rearrange("p (c d) -> p c d", c=CH) for _ in range(2)]
        dst_hot = [inside(CH * W1).rearrange("p (c w) -> p c w", c=CH) for _ in range(2)]
        ea_left = [inside(SG, RK) for _ in range(2)]
        ea_round = [counts_even[0:RK, :, :].rearrange("p a b -> p (a b)").bitcast(bf16)[:, n * SG:(n + 1) * SG] for n in range(2)]
        ea_mid = [counts_even[0:RK, :, :].rearrange("p a b -> p (a b)").bitcast(bf16)[:, n * SG:(n + 1) * SG] for n in range(2, 4)]
        ea_parts = [low_hot[0:RK, n, :, :, :].rearrange("p a b c -> p (a b c)") for n in range(2)]
        gathered = sb("gathered", [P, SLOTS, CH, D], fp32)
        ea_sb = sb("ea_sb", [RK, SLOTS, SG], fp32)
        hidden = sb("hidden", [DE, 2, SG], fp32)
        index = sb("index", [P, SLOTS, CH], i32)
        last_src = sb("last_src", [NS, P], i32)
        last_near = sb("last_near", [NS, P], fp16)
        src_row = sb("src_row", [P, SLOTS, P], fp16)
        iota_node = sb("iota_node", [P, NT, IC], fp16)
        counts_odd = (gathered[:, :, :, :].rearrange("p a b c -> p (a b c)").bitcast(fp16)[:, 0:NT * B0 * VC]
                      .rearrange("p (a b) -> p a b", a=NT))
        counts = (counts_even, counts_odd)
        early = gathered[:, :, :, :].rearrange("p a b c -> p (a b c)")
        node_hot = [tile[:, :, :].rearrange("p t d -> p (t d)").bitcast(bf16)[:, 0:NT * P].rearrange("p (t e) -> p t e", t=NT)
                    for tile in (y, x_sb)]
        x1_left = y
        x1_part = xs_part[:, :, :, 0:D]
        part_127 = early[:, 0:NC].bitcast(i32)
        lo_hot = early[:, NC:NC + LO * HC].bitcast(bf16).rearrange("p (n j a b) -> p n j a b", n=2, j=HC // IC, b=IC)
        hi_hot = early[:, NC + LO * HC:NC + (LO + HI) * HC].bitcast(bf16).rearrange("p (n j a b) -> p n j a b", n=2, j=HC // IC, b=IC)

        bank = [ctx.enter_context(nc.psum_tensor(f"bank{i}", [P, 512], fp32)) for i in range(8)]

        src_in, dst_in, nodes_in, weights_in = sem("src_in"), sem("dst_in"), sem("nodes_in"), sem("weights_in")
        late_const, bias_added = sem("late_const"), sem("bias_added")
        const_ready, ident_zero = sem("const_ready"), sem("ident_zero")
        v_step, sweep_step, fold_step = sem("v_step"), sem("sweep_step"), sem("fold_step")
        carrier = sem("carrier")
        xw_made, xw_taken = sem("xw_made"), sem("xw_taken")
        diag_ready, bases_spread, sweeps_ready = sem("diag_ready"), sem("bases_spread"), sem("sweeps_ready")
        hist_ready, hist_used, hist_done = sem("hist_ready"), sem("hist_used"), sem("hist_done")
        deg_ready, root_ready = sem("deg_ready"), sem("root_ready")
        inverse_ready, left_made, part_rounded, xs_ready = sem("inverse_ready"), sem("left_made"), sem("part_rounded"), sem("xs_ready")
        hots_ready = sem("hots_ready")
        counts_made = [sem(f"counts_made{i}") for i in range(4)]
        counts_taken = [sem(f"counts_taken{i}") for i in range(4)]
        sums_made, sums_taken, window_added = sem("sums_made"), sem("sums_taken"), sem("window_added")
        bases0_ready, bases0_used = sem("bases0_ready"), sem("bases0_used")
        layer0_done = sem("layer0_done")
        agg_made = sem("agg_made")
        var_ready, std_ready = sem("var_ready"), sem("std_ready")
        x1_ready, x1_ready_act = sem("x1_ready"), sem("x1_ready_act")
        x1_stored, x1_stored_pool = sem("x1_stored"), sem("x1_stored_pool")
        shift_ready, y_ready, y_ready_act = sem("shift_ready"), sem("y_ready"), sem("y_ready_act")
        turned, turn_taken, self_made, self_taken = sem("turned"), sem("turn_taken"), sem("self_made"), sem("self_taken")
        attrs_in = [sem(f"attrs_in{i}") for i in range(SLOTS)]
        index_in = [sem(f"index_in{i}") for i in range(SLOTS)]
        last_src_in, near_made, near_stored = sem("last_src_in"), sem("near_made"), sem("near_stored")
        src_row_in = [sem(f"src_row_in{i}") for i in range(SLOTS)]
        x1_rounded, x1_left_made, node_hot_ready = sem("x1_rounded"), sem("x1_left_made"), sem("node_hot_ready")
        last_rows_in = sem("last_rows_in")
        rows_in = [[sem(f"rows_in{i}_{h}") for h in range(2)] for i in range(SLOTS)]
        rounded, left_ready = sem("rounded"), sem("left_ready")
        mid_ready, parts_ready = sem("mid_ready"), sem("parts_ready")
        hidden_made, hidden_ready = sem("hidden_made"), sem("hidden_ready")
        weights_made, messages_ready = sem("weights_made"), sem("messages_ready")
        hot_ready, window_made, window_taken = sem("hot_ready"), sem("window_made"), sem("window_taken")
        layer1_done, sums1_made = sem("layer1_done"), sem("sums1_made")
        out_stored = sem("out_stored")

        def counter(engine, own):
            total = [0]

            def step():
                total[0] += 1
                return 1

            return step, lambda: engine.wait_ge(own, total[0])

        def x1_rows(g):
            return x1_table[g * BT * P:(g + 1) * BT * P, :].rearrange("(t p) d -> p t d", p=P)

        CONSTS, LATE = 7, 9
        rounds = NS // SLOTS
        per_slot = [rounds + (slot < NS % SLOTS) for slot in range(SLOTS)]
        assert NS % SLOTS == NS % B0 == NB % 2 == 1

        block = ctx.enter_context(nc.Block())

        @block.sync
        def _(sp):
            sp.dma_start(src_i[:, :], src_pm).then_inc(src_in, 16)
            sp.dma_start(dst_r, dst_rows).then_inc(dst_in, 16)
            sp.dma_start(dst_i[:, :], dst_pm).then_inc(dst_in, 16)
            sp.dma_start(last_src[:, :], src_rows[:, SG - P:SG]).then_inc(last_src_in, 16)
            sp.dma_start(x_sb[:, :, :], x_rows.rearrange("(t p) d -> p t d", p=P)).then_inc(nodes_in, 16)
            sp.dma_start(b0_sb[:, :], b0.broadcast_to([P, D])).then_inc(nodes_in, 16)
            for tile, source in ((w0_sb, w0e), (w1_rep, w1t), (masks, part_masks), (b1_sb, b1c), (w2_sb, w2e), (ws_sb, wse),
                                 (wn_sb, wnt), (xT, x_cols)):
                sp.dma_start(tile[:, :], source).then_inc(weights_in, 16)

            sp.wait_ge(near_stored, 16)
            sp.wait_ge(sweeps_ready, 1)
            n_sweeps = sp.value_load(sweeps_i[0:1, 1:2], min_val=1, max_val=SWEEPS1)

            def load(sweep, i, slot):
                n = sweep * NS + i
                sp.wait_ge(left_ready, n + 1)
                sp.dma_start(ea_sb[:, slot, :], ea_cols[:, bass.ds(i * SG, SG)]).then_inc(attrs_in[slot], 16)
                sp.wait_ge(messages_ready, n * 2 + 2)
                sp.dma_start(index[:, slot, :], src_pm[:, bass.ds(i * CH, CH)]).then_inc(index_in[slot], 16)
                sp.dma_start(src_row[:, slot, :], src_near[bass.ds(i, 1), :].broadcast_to([P, P])).then_inc(src_row_in[slot], 16)

            with sp.Fori(0, n_sweeps) as sweep:
                sp.wait_ge(left_ready, sweep * NS + 4)
                sp.sem_inc(carrier, 1)
                sp.wait_ge(messages_ready, sweep * (NS * 2) + 8)
                sp.sem_inc(carrier, 1)
                with sp.Fori(0, rounds) as k:
                    for slot in range(SLOTS):
                        load(sweep, k * SLOTS + slot, slot)
                load(sweep, NS - 1, 0)

            for g in range(DVE_GROUPS):
                rows = min((g + 1) * BT, NODES // P) - g * BT
                sp.wait_ge(y_ready, g + 1)
                sp.dma_start(out[g * BT * P:(g * BT + rows) * P, :].rearrange("(t p) d -> p t d", p=P),
                             y[:, g * BT:g * BT + rows, :]).then_inc(out_stored, 16)
            last = NODES // P
            sp.wait_ge(y_ready_act, TB - DVE_GROUPS)
            sp.dma_start(out[last * P:NODES, :], y[0:NODES - last * P, last, :]).then_inc(out_stored, 16)
            sp.wait_ge(out_stored, (TB + 1) * 16)

        @block.gpsimd
        def _(pool):
            def numbers(tile, pattern):
                return pool.iota(tile, pattern, base=0, channel_multiplier=0, allow_small_or_imprecise_dtypes=True)

            numbers(iota_low[:, :, :], [[1, P], [0, IC]]).then_inc(const_ready, 1)
            pool.memset(zeros[:, :], 0.0).then_inc(const_ready, 1)
            pool.memset(ident[:, :], 0.0).then_inc(ident_zero, 1)
            pool.memset(ones[:, :], 1.0).then_inc(const_ready, 1)
            pool.wait_ge(ident_zero, 1)
            pool.affine_select(out=ident[:, :], in_=ident[:, :], compare_op=ALU.not_equal, fill=1.0, base=0,
                               pattern=[[-1, P]], channel_multiplier=1).then_inc(const_ready, 1)
            numbers(iota_sw[:, 0:SWEEPS0], [[W0, SWEEPS0]]).then_inc(const_ready, 1)
            numbers(iota_sw[:, SWEEPS0:], [[W1, SWEEPS1]]).then_inc(const_ready, 1)
            numbers(iota_key[:, :, :, :], [[1, NT], [NT, W0], [0, IC]]).then_inc(const_ready, 1)
            numbers(iota_w1[:, :], [[1, W1]]).then_inc(late_const, 1)
            pool.memset(xs_part[:, 0, :, D:DE], 1.0).then_inc(late_const, 1)
            pool.memset(xs_part[:, 1:3, :, D:DE], 0.0).then_inc(late_const, 1)
            pool.memset(agg0T[:, :], 0.0).then_inc(late_const, 1)
            pool.memset(agg1T[:, :], 0.0).then_inc(late_const, 1)
            pool.iota(iota_node[:, :, :], [[P, NT], [0, IC]], base=-MIDDLE, channel_multiplier=1,
                      allow_small_or_imprecise_dtypes=True).then_inc(late_const, 1)
            pool.wait_ge(last_src_in, 16)
            pool.tensor_scalar(out=last_near[:, :], in0=last_src[:, :], scalar1=-float(MIDDLE), scalar2=None,
                               op0=ALU.add).then_inc(near_made, 1)
            pool.wait_ge(near_made, 1)
            pool.dma_start(src_near, last_near[:, :]).then_inc(near_stored, 16)
            pool.wait_ge(nodes_in, 32)
            pool.tensor_tensor(out=y[:, :, :], in0=x_sb[:, :, :], in1=b0_sb[:, :].unsqueeze(1).broadcast_to([P, NT, D]),
                               op=ALU.add).then_inc(bias_added, 1)
            pool.wait_ge(late_const, 6)
            pool.wait_ge(bias_added, 1)
            pool.memset(x1T[D:D + 2, :], 1.0).then_inc(late_const, 1)
            pool.memset(hidden[D:DE, :, :], 1.0).then_inc(late_const, 1)
            pool.wait_ge(late_const, 8)
            pool.sem_inc(late_const, 1)

            halves = (slice(0, NT // 2), slice(NT // 2, NT))
            pool.wait_ge(inverse_ready, 1)
            for h, tiles in enumerate(halves):
                pool.tensor_tensor(out=xs[:, tiles, :], in0=x_sb[:, tiles, :],
                                   in1=deg[:, 2, tiles].unsqueeze(2).broadcast_to([P, tiles.stop - tiles.start, D]),
                                   op=ALU.mult).then_inc(left_made, 1)
            for h, tiles in enumerate(halves):
                pool.wait_ge(part_rounded, h + 1)
                pool.tensor_tensor(out=xs[:, tiles, :], in0=xs[:, tiles, :], in1=xs_part[:, 0, tiles, 0:D],
                                   op=ALU.subtract).then_inc(left_made, 1)
            for h, tiles in enumerate(halves):
                pool.wait_ge(part_rounded, h + 3)
                pool.tensor_tensor(out=xs_part[:, 2, tiles, 0:D], in0=xs[:, tiles, :], in1=xs_part[:, 1, tiles, 0:D],
                                   op=ALU.subtract).then_inc(xs_ready, 1)

            pool.wait_ge(sweeps_ready, 1)
            n_sweeps = pool.value_load(sweeps_i[0:1, 0:1], min_val=1, max_val=SWEEPS0)
            pool.sem_inc(window_added, 1)
            pool.sem_inc(bases0_used, 1)

            def add_windows(sweep, b):
                first_window = sweep * (NS * NG) + b * (B0 * NG)
                pool.wait_ge(sums_taken, sweep * (NB + 1) + b + 3)
                pool.sem_inc(carrier, 1)
                for some in range(0, B0 * NG, 2 * NG):
                    these = range(some, some + 2 * NG)
                    bases = []
                    for g in these[::NG]:
                        bases += nc.values_load_multi_w_load_instructions(
                            base0_i[0:1, bass.ds(b * (B0 * NG) + g, NG)], [mybir.EngineType.Pool], min_val=0, max_val=NP,
                            skip_runtime_bounds_check_because="the bases are clamped on the chip")[1]
                    for g, base in zip(these, bases):
                        pool.wait_ge(window_added, first_window + g + 1)
                        pool.sem_inc(carrier, 1)
                        window = agg0T[:, bass.ds(base, W0)]
                        pool.tensor_tensor(out=window, in0=window, in1=window_sums[:, g * W0:(g + 1) * W0],
                                           op=ALU.add).then_inc(window_added, 1)

            with pool.Fori(0, n_sweeps) as sweep:
                pool.wait_ge(bases0_ready, sweep + 1)
                pool.sem_inc(carrier, 1)
                with pool.Fori(0, NB - 1) as b:
                    add_windows(sweep, b)
                pool.sem_inc(bases0_used, 1)
            pool.wait_ge(window_added, n_sweeps * (NS * NG) + 1)
            pool.sem_inc(layer0_done, 1)

            for g in range(DVE_GROUPS):
                pool.wait_ge(x1_ready, g + 1)
                pool.dma_start(x1_rows(g), x1[:, g * BT:(g + 1) * BT, :]).then_inc(x1_stored_pool, 16)
            n_sweeps = pool.value_load(sweeps_i[0:1, 1:2], min_val=1, max_val=SWEEPS1)
            pool.wait_ge(x1_stored_pool, DVE_GROUPS * 16)
            pool.wait_ge(x1_stored, (TB - DVE_GROUPS) * 16)

            def gather(sweep, i, slot, nth):
                pool.wait_ge(messages_ready, (sweep * NS + i) * 2 + 2)
                pool.sem_inc(carrier, 1)
                pool.wait_ge(index_in[slot], (nth + 1) * 16)
                pool.sem_inc(carrier, 1)
                for c in range(DENSE):
                    pool.indirect_dma_start(out=gathered[:, slot, c, :], out_offset=None, in_=x1_table,
                                            in_offset=bass.IndirectOffsetOnAxis(ap=index[:, slot, c:c + 1], axis=0),
                                            ).then_inc(rows_in[slot][c * 2 // CH], 16)

            with pool.Fori(0, n_sweeps) as sweep:
                pool.wait_ge(messages_ready, sweep * (NS * 2) + 8)
                pool.sem_inc(carrier, 1)
                with pool.Fori(0, rounds) as k:
                    for slot in range(SLOTS):
                        gather(sweep, k * SLOTS + slot, slot, sweep * per_slot[slot] + k)
                gather(sweep, NS - 1, 0, sweep * per_slot[0] + rounds)

        @block.vector
        def _(ve):
            step, settle = counter(ve, v_step)

            ve.sem_inc(messages_ready, 8)
            ve.sem_inc(left_ready, 4)

            ve.wait_ge(src_in, 16)
            for part, op, by in ((part_6, ALU.logical_shift_right, 6), (part_63, ALU.bitwise_and, LO - 1),
                                 (part_7, ALU.logical_shift_right, 7), (part_127, ALU.bitwise_and, P - 1)):
                ve.tensor_scalar(out=part, in0=src_i[:, :], scalar1=by, scalar2=None, op0=op).then_inc(v_step, step())
            settle()
            ve.tensor_copy(high6[:, :], part_6).then_inc(v_step, step())
            ve.tensor_copy(low6[:, :], part_63).then_inc(v_step, step())
            ve.tensor_copy(low7[:, :], part_127).then_inc(v_step, step())
            settle()
            ve.wait_ge(const_ready, CONSTS)

            def one_hot(hot, numbers, values):
                shape = list(hot.shape)
                return ve.tensor_tensor(out=hot, in0=numbers.unsqueeze(1).broadcast_to(shape),
                                        in1=values.rearrange("p (j i) -> p j i", i=IC).unsqueeze(2).broadcast_to(shape),
                                        op=ALU.is_equal)

            def hist(n, slot, chunks=HC):
                ve.wait_ge(hist_used, n + 1)
                for hot, width, part in ((lo_hot, LO, low6), (hi_hot, HI, high6)):
                    made = one_hot(hot[:, slot, 0:chunks // IC, :, :], iota_low[:, 0:width, :], part[:, bass.ds(n * HC, chunks)])
                made.then_inc(hist_ready, 1)

            with ve.Fori(0, HISTS // HIST_UNROLL) as k:
                for m in range(HIST_UNROLL):
                    hist(k * HIST_UNROLL + m, m % 2)
            for n in range(HISTS // HIST_UNROLL * HIST_UNROLL, HISTS):
                hist(n, n % 2)
            hist(HISTS, HISTS % 2, CH)

            def inverse_root(of, root, inv, tmp):
                ve.reciprocal(inv, root).then_inc(v_step, step())
                settle()
                ve.tensor_tensor(out=tmp, in0=inv, in1=inv, op=ALU.mult).then_inc(v_step, step())
                settle()
                ve.tensor_tensor(out=tmp, in0=tmp, in1=of, op=ALU.mult).then_inc(v_step, step())
                settle()
                ve.tensor_scalar(out=tmp, in0=tmp, scalar1=-0.5, scalar2=1.5, op0=ALU.mult, op1=ALU.add).then_inc(v_step, step())
                settle()
                ve.tensor_tensor(out=inv, in0=inv, in1=tmp, op=ALU.mult).then_inc(v_step, step())
                settle()

            ve.wait_ge(hist_done, 1)
            pairs = bank[1][0:LO, 0:HI].rearrange("p (t two) -> p t two", two=2)
            for half in range(2):
                ve.tensor_scalar(out=deg[half * LO:(half + 1) * LO, 0, :], in0=pairs[:, :, half], scalar1=1.0, scalar2=None,
                                 op0=ALU.max).then_inc(v_step, step())
            settle()
            ve.sem_inc(deg_ready, 1)

            ve.wait_ge(dst_in, 32)
            bases, ends, lengths = stats[:, 0:NG], stats[:, 8:8 + NG], stats[:, 12:12 + NG]
            base_all, widest, length_all, end_all = (stats[:, n:n + 1] for n in range(NG, NG + 4))
            ve.tensor_reduce(out=bases, in_=dst_r.rearrange("p (g e) -> p g e", g=NG), axis=AX.X, op=ALU.min).then_inc(v_step, step())
            ve.scalar_tensor_tensor(out=masked, in0=dst_r, scalar=float(NP), in1=dst_r, op0=ALU.is_lt,
                                    op1=ALU.mult).then_inc(v_step, step())
            ve.wait_ge(root_ready, 1)
            inverse_root(deg[:, 0, :], deg[:, 1, :], deg[:, 2, :], deg[:, 3, :])
            ve.sem_inc(inverse_ready, 1)
            ve.tensor_reduce(out=ends, in_=masked.rearrange("p (g e) -> p g e", g=NG), axis=AX.X, op=ALU.max).then_inc(v_step, step())
            ve.tensor_scalar(out=bases, in0=bases, scalar1=float(NP), scalar2=None, op0=ALU.min).then_inc(v_step, step())
            settle()
            ve.tensor_reduce(out=base_all, in_=bases, axis=AX.X, op=ALU.min).then_inc(v_step, step())
            ve.tensor_tensor(out=lengths, in0=ends, in1=bases, op=ALU.subtract).then_inc(v_step, step())
            ve.tensor_reduce(out=end_all, in_=ends, axis=AX.X, op=ALU.max).then_inc(v_step, step())
            settle()
            ve.tensor_reduce(out=widest, in_=lengths, axis=AX.X, op=ALU.max).then_inc(v_step, step())
            ve.tensor_tensor(out=length_all, in0=end_all, in1=base_all, op=ALU.subtract).then_inc(v_step, step())
            settle()
            for col in range(NG + 3):
                made = ve.tensor_scalar(out=diag[:, col, :], in0=ident[0:NS, 0:NS], scalar1=stats[:, col:col + 1],
                                        scalar2=None, op0=ALU.mult)
            made.then_inc(diag_ready, 1)
            ve.wait_ge(bases_spread, 1)
            spread = [bank[2 + col // 4][:, col % 4 * NS:(col % 4 + 1) * NS] for col in range(NG + 3)]
            dst_g = dst_i[:, :].rearrange("p (s g c) -> p s g c", g=NG, c=GC)
            key_g = key[:, :].rearrange("p (s g c) -> p s g c", g=NG, c=GC)
            for g in range(NG):
                ve.tensor_tensor(out=key_g[:, :, g, :], in0=dst_g[:, :, g, :],
                                 in1=spread[g].unsqueeze(2).broadcast_to([P, NS, GC]),
                                 op=ALU.subtract).then_inc(v_step, step())
            ve.tensor_tensor(out=rel1[:, :].rearrange("p (s c) -> p s c", c=CH),
                             in0=dst_i[:, :].rearrange("p (s c) -> p s c", c=CH),
                             in1=spread[NG].unsqueeze(2).broadcast_to([P, NS, CH]),
                             op=ALU.subtract).then_inc(v_step, step())
            for g in range(NG):
                ve.tensor_copy(base0_f[:, :, g], spread[g][0:1, :]).then_inc(v_step, step())
            ve.tensor_copy(base1_f[:, :], spread[NG][0:1, :]).then_inc(v_step, step())
            for n in range(2):
                ve.tensor_reduce(out=spans[:, n:n + 1], in_=spread[NG + 1 + n][0:1, :], axis=AX.X,
                                 op=ALU.max).then_inc(v_step, step())
            settle()
            ve.scalar_tensor_tensor(out=key[:, :], in0=key[:, :], scalar=float(NT), in1=part_7,
                                    op0=ALU.mult, op1=ALU.add).then_inc(v_step, step())
            for n, (a, z) in enumerate(((0, SWEEPS0), (SWEEPS0, SWEEPS0 + SWEEPS1))):
                ve.tensor_scalar(out=within[:, a:z], in0=iota_sw[:, a:z], scalar1=spans[:, n:n + 1], scalar2=None,
                                 op0=ALU.is_le).then_inc(v_step, step())
            settle()
            for n, (a, z) in enumerate(((0, SWEEPS0), (SWEEPS0, SWEEPS0 + SWEEPS1))):
                ve.tensor_reduce(out=sweeps_f[:, n:n + 1], in_=within[:, a:z], axis=AX.X, op=ALU.add).then_inc(v_step, step())
            settle()
            ve.tensor_scalar(out=sweeps_i[:, :], in0=sweeps_f[:, :], scalar1=1.0, scalar2=None,
                             op0=ALU.max).then_inc(sweeps_ready, 1)

            ve.wait_ge(sweeps_ready, 1)
            n_sweeps = ve.value_load(sweeps_i[0:1, 0:1], min_val=1, max_val=SWEEPS0)

            def one_hots(sweep, s, q):
                ve.wait_ge(counts_taken[NG - 1], sweep * NS + s + 1)
                one_hot(key_hot[:, q, :, :, :], iota_key[:, :, :, :].rearrange("p a b i -> p (a b) i"), key_near[:, bass.ds(s * CH, CH)])
                one_hot(low_hot[:, q, :, :, :], iota_low[:, :, :], low7[:, bass.ds(s * CH, CH)]).then_inc(hots_ready, 1)

            def add_windows(sweep, b, supers):
                first_window = sweep * (NS * NG) + b * (B0 * NG)
                bases = []
                for q in range(supers):
                    bases += nc.values_load_multi_w_load_instructions(
                        base0_i[0:1, bass.ds((b * B0 + q) * NG, NG)], [mybir.EngineType.DVE], min_val=0, max_val=NP,
                        skip_runtime_bounds_check_because="the bases are clamped on the chip")[1]
                ve.wait_ge(sums_taken, sweep * (NB + 1) + b + 3)
                for g, base in enumerate(bases):
                    ve.wait_ge(window_added, first_window + g + 1)
                    window = agg0T[:, bass.ds(base, W0)]
                    ve.tensor_tensor(out=window, in0=window, in1=window_sums[:, g * W0:(g + 1) * W0],
                                     op=ALU.add).then_inc(window_added, 1)

            with ve.Fori(0, n_sweeps) as sweep:
                ve.wait_ge(bases0_used, sweep + 1)
                ve.wait_ge(counts_taken[NG - 1], sweep * NS + B0)
                ve.tensor_scalar(out=base0_c[:, :], in0=base0_f[:, :, :].rearrange("p s g -> p (s g)"), scalar1=float(NP),
                                 scalar2=None, op0=ALU.min).then_inc(sweep_step, 1)
                ve.tensor_scalar(out=key_near[:, :], in0=key[:, :], scalar1=2000.0, scalar2=-2000.0, op0=ALU.min,
                                 op1=ALU.max).then_inc(sweep_step, 1)
                ve.wait_ge(sweep_step, sweep * 4 + 2)
                ve.tensor_copy(base0_i[:, :], base0_c[:, :]).then_inc(bases0_ready, 1)
                with ve.Fori(0, NB) as b:
                    for q in range(B0):
                        one_hots(sweep, b * B0 + q, q)
                one_hots(sweep, NS - 1, 0)
                ve.wait_ge(bases0_ready, sweep + 1)
                ve.sem_inc(carrier, 1)
                add_windows(sweep, NB - 1, B0)
                add_windows(sweep, NB, NS - NB * B0)
                ve.wait_ge(hots_ready, (sweep + 1) * NS)
                ve.tensor_scalar(out=key[:, :], in0=key[:, :], scalar1=-float(KEYS), scalar2=None,
                                 op0=ALU.add).then_inc(sweep_step, 1)
                ve.tensor_scalar(out=base0_f[:, :, :], in0=base0_f[:, :, :], scalar1=float(W0), scalar2=None,
                                 op0=ALU.add).then_inc(sweep_step, 1)
                ve.wait_ge(sweep_step, sweep * 4 + 4)

            mean, half_gap, scatter, variance = (norms[:, n, :] for n in range(4))
            inverse, shift = deg[:, 2, :], norms[:, 4, :]

            def tiles_of(g):
                return slice(g * BT, (g + 1) * BT)

            def in_bank(b):
                return bank[b][:, 0:BT * D].rearrange("p (t d) -> p t d", t=BT)

            def tile_stats(source, g):
                for t in range(g * BT, (g + 1) * BT):
                    ve.bn_stats(out=bn6[:, t, :], in_=source[:, t, :]).then_inc(v_step, step())

            def norm(target, source, ready, nth):
                settle()
                ve.tensor_tensor(out=mean, in0=bn6[:, :, 1], in1=bn6[:, :, 4], op=ALU.add).then_inc(v_step, step())
                ve.tensor_tensor(out=half_gap, in0=bn6[:, :, 1], in1=bn6[:, :, 4], op=ALU.subtract).then_inc(v_step, step())
                ve.tensor_tensor(out=scatter, in0=bn6[:, :, 2], in1=bn6[:, :, 5], op=ALU.add).then_inc(v_step, step())
                settle()
                ve.tensor_scalar(out=mean, in0=mean, scalar1=0.5, scalar2=None, op0=ALU.mult).then_inc(v_step, step())
                ve.scalar_tensor_tensor(out=half_gap, in0=half_gap, scalar=0.25, in1=half_gap, op0=ALU.mult,
                                        op1=ALU.mult).then_inc(v_step, step())
                ve.tensor_scalar(out=scatter, in0=scatter, scalar1=1.0 / D, scalar2=EPS, op0=ALU.mult,
                                 op1=ALU.add).then_inc(v_step, step())
                settle()
                ve.tensor_tensor(out=variance, in0=scatter, in1=half_gap, op=ALU.add).then_inc(v_step, step())
                settle()
                ve.sem_inc(var_ready, 1)
                ve.wait_ge(std_ready, nth)
                inverse_root(variance, deg[:, 1, :], inverse, deg[:, 3, :])
                ve.scalar_tensor_tensor(out=shift, in0=mean, scalar=-1.0, in1=inverse, op0=ALU.mult,
                                        op1=ALU.mult).then_inc(shift_ready, 1)
                for g in range(DVE_GROUPS):
                    for t in range(g * BT, (g + 1) * BT):
                        ve.tensor_scalar(out=target[:, t, :], in0=source[:, t, :], scalar1=mean[:, t:t + 1],
                                         scalar2=inverse[:, t:t + 1], op0=ALU.subtract,
                                         op1=ALU.mult).then_inc(ready if t % BT == BT - 1 else v_step,
                                                                1 if t % BT == BT - 1 else step())

            in_banks = [bank[1 + g][:, 0:BT * DE].rearrange("p (t d) -> p t d", t=BT) for g in range(TB)]
            ve.wait_ge(xw_taken, TB)
            ve.wait_ge(bias_added, 1)
            for g in range(TB):
                ve.wait_ge(agg_made, g + 1)
                in_degree = in_banks[g][:, :, D]
                ve.tensor_scalar(out=deg[:, 0, tiles_of(g)], in0=in_degree, scalar1=1.0, scalar2=None, op0=ALU.max).then_inc(v_step, step())
                ve.tensor_scalar(out=deg[:, 4, tiles_of(g)], in0=in_degree, scalar1=0.0, scalar2=None, op0=ALU.is_equal).then_inc(v_step, step())
                settle()
                if g == TB - 1:
                    ve.sem_inc(deg_ready, 1)
                for t in range(g * BT, (g + 1) * BT):
                    ve.scalar_tensor_tensor(out=xw[:, t, :], in0=xw[:, t, :], scalar=deg[:, 4, t:t + 1], in1=y[:, t, :],
                                            op0=ALU.mult, op1=ALU.add).then_inc(v_step, step())
            ve.wait_ge(root_ready, 2)
            inverse_root(deg[:, 0, :], deg[:, 1, :], inverse, deg[:, 3, :])
            for g in range(TB):
                for t in range(g * BT, (g + 1) * BT):
                    ve.scalar_tensor_tensor(out=xw[:, t, :], in0=in_banks[g][:, t % BT, 0:D], scalar=inverse[:, t:t + 1],
                                            in1=xw[:, t, :], op0=ALU.mult, op1=ALU.add).then_inc(v_step, step())
            settle()
            for g in range(TB):
                tile_stats(xw, g)
            norm(x1, xw, x1_ready, 1)

            n_sweeps = ve.value_load(sweeps_i[0:1, 1:2], min_val=1, max_val=SWEEPS1)
            ve.sem_inc(window_taken, 2)
            ve.sem_inc(parts_ready, 1)
            ve.wait_ge(x1_rounded, 1)
            ve.tensor_tensor(out=x1_left[:, :, :], in0=x1[:, :, :], in1=x1_part[:, 0, :, :], op=ALU.subtract).then_inc(x1_left_made, 1)
            ve.wait_ge(weights_in, 8 * 16)
            piece = [messages[0][0:RK, n, :] for n in range(3)]
            for n in range(3):
                ve.tensor_copy(w1_sb[:, 0, :], w1_rep[:, :]).then_inc(v_step, step())
                settle()
                ve.tensor_copy(piece[n], w1_sb[:, 0, :]).then_inc(v_step, step())
                ve.tensor_tensor(out=w1_rep[:, :], in0=w1_rep[:, :], in1=w1_sb[:, 0, :],
                                 op=ALU.subtract).then_inc(v_step, step())
                settle()
            for half in range(2):
                for n in range(3):
                    ve.scalar_tensor_tensor(out=w1_sb[:, half, :], in0=piece[n], scalar=masks[:, 2 + 3 * half + n:3 + 3 * half + n],
                                            in1=w1_rep[:, :] if n == 0 else w1_sb[:, half, :],
                                            op0=ALU.mult, op1=ALU.add).then_inc(v_step, step())
                    settle()

            ve.wait_ge(x1_rounded, 2)
            ve.tensor_tensor(out=x1_part[:, 2, :, :], in0=x1_left[:, :, :], in1=x1_part[:, 1, :, :], op=ALU.subtract).then_inc(v_step, step())
            settle()

            def find_nodes(slot, nth):
                shape = [P, NT, P // IC, IC]
                ve.wait_ge(src_row_in[slot], (nth + 1) * 16)
                ve.tensor_tensor(out=node_hot[slot % 2].rearrange("p t (j i) -> p t j i", i=IC),
                                 in0=src_row[:, slot, :].rearrange("p (j i) -> p j i", i=IC).unsqueeze(1).broadcast_to(shape),
                                 in1=iota_node[:, :, :].unsqueeze(2).broadcast_to(shape), op=ALU.is_equal).then_inc(node_hot_ready, 1)

            def less_first(n, slot, place):
                ve.wait_ge(rounded, n + 1)
                ve.wait_ge(parts_ready, n + 1)
                ve.scalar_tensor_tensor(out=ea_left[place], in0=ea_round[place], scalar=masks[:, 0:1], in1=ea_sb[:, slot, :],
                                        op0=ALU.mult, op1=ALU.add).then_inc(left_ready, 1)

            def split(n, place):
                ve.wait_ge(mid_ready, n + 1)
                ve.scalar_tensor_tensor(out=ea_parts[place], in0=ea_mid[place], scalar=masks[:, 1:2], in1=ea_left[place],
                                        op0=ALU.mult, op1=ALU.add).then_inc(parts_ready, 1)

            def place_edges(sweep, i, place):
                ve.wait_ge(window_made, sweep * NS + i + 1)
                ve.tensor_tensor(out=dst_hot[place], in0=iota_w1[:, :].unsqueeze(1).broadcast_to([P, CH, W1]),
                                 in1=rel1[:, bass.ds(i * CH, CH)].unsqueeze(2).broadcast_to([P, CH, W1]),
                                 op=ALU.is_equal).then_inc(hot_ready, 1)

            def fold(sweep, i, slot, k, left=2):
                n, nth = sweep * NS + i, sweep * per_slot[slot] + k
                base = ve.value_load(base1_i[0:1, bass.ds(i, 1)], min_val=0, max_val=NP)
                for h in range(2):
                    dense = h == DENSE * 2 // CH
                    half = slice(h * CH // 2, (h + 1) * CH // 2)
                    weights = bank[2 + 2 * (slot % 2) + h]
                    ve.wait_ge(rows_in[slot][h], (nth + 1) * ((CH // 2 - dense) * 16))
                    ve.wait_ge(weights_made, n * 2 + h + 5)
                    if dense:
                        ve.tensor_copy(gathered[:, slot, DENSE, :], weights[:, CH // 2 * D:(CH // 2 + 1) * D]).then_inc(last_rows_in, 1)
                        ve.wait_ge(last_rows_in, n + 1)
                    ve.tensor_tensor(out=messages[slot % 2][:, half, :],
                                     in0=weights[:, 0:CH // 2 * D].rearrange("p (c d) -> p c d", d=D),
                                     in1=gathered[:, slot, half, :], op=ALU.mult).then_inc(messages_ready, 1)
                second = (slot + 2) % SLOTS
                if left >= 2:
                    less_first(n + 2, second, slot % 2)
                    find_nodes(second, sweep * per_slot[second] + k + (slot + 2) // SLOTS)
                if left >= 1:
                    place_edges(sweep, i + 1, (slot + 1) % 2)
                if left >= 2:
                    split(n + 2, slot % 2)
                ve.wait_ge(window_made, n + 3)
                ve.wait_ge(window_taken, n + 2)
                window = agg1T[0:D, bass.ds(base, W1)]
                ve.tensor_tensor(out=window, in0=window, in1=bank[6 + slot % 2][0:D, 0:W1], op=ALU.add).then_inc(window_taken, 1)

            with ve.Fori(0, n_sweeps) as sweep:
                ve.wait_ge(window_made, sweep * NS + 2)
                ve.tensor_scalar(out=base1_c[:, :], in0=base1_f[:, :], scalar1=float(NP), scalar2=None,
                                 op0=ALU.min).then_inc(fold_step, 1)
                ve.wait_ge(fold_step, sweep * 4 + 1)
                ve.tensor_copy(base1_i[:, :], base1_c[:, :]).then_inc(fold_step, 1)
                ve.wait_ge(fold_step, sweep * 4 + 2)
                ve.sem_inc(carrier, 1)
                for first in range(2):
                    less_first(sweep * NS + first, first, first)
                    split(sweep * NS + first, first)
                for first in range(2):
                    find_nodes(first, sweep * per_slot[first])
                place_edges(sweep, 0, 0)
                with ve.Fori(0, rounds - 1) as k:
                    for slot in range(SLOTS):
                        fold(sweep, k * SLOTS + slot, slot, k)
                for i in range(NS - 1 - SLOTS, NS):
                    fold(sweep, i, i % SLOTS, i // SLOTS, min(2, NS - 1 - i))
                ve.wait_ge(hot_ready, (sweep + 1) * NS)
                ve.tensor_scalar(out=rel1[:, :], in0=rel1[:, :], scalar1=-float(W1), scalar2=None,
                                 op0=ALU.add).then_inc(fold_step, 1)
                ve.tensor_scalar(out=base1_f[:, :], in0=base1_f[:, :], scalar1=float(W1), scalar2=None,
                                 op0=ALU.add).then_inc(fold_step, 1)
                ve.wait_ge(fold_step, sweep * 4 + 4)
            ve.wait_ge(window_taken, n_sweeps * NS + 2)
            ve.sem_inc(layer1_done, 1)

            ve.wait_ge(self_taken, TB)
            for g in range(TB):
                ve.wait_ge(sums1_made, g + 1)
                ve.tensor_tensor(out=xw[:, tiles_of(g), :], in0=xw[:, tiles_of(g), :], in1=in_bank(g),
                                 op=ALU.add).then_inc(v_step, step())
                settle()
                ve.scalar_tensor_tensor(out=xw[:, tiles_of(g), :], in0=xw[:, tiles_of(g), :], scalar=0.0,
                                        in1=x1[:, tiles_of(g), :], op0=ALU.max, op1=ALU.add).then_inc(v_step, step())
                settle()
                tile_stats(xw, g)
            norm(y, xw, y_ready, 2)

        @block.scalar
        def _(ac):
            def to_xw(g, b, done):
                ac.activation(xw[:, g * BT:(g + 1) * BT, :], bank[b][:, 0:BT * D].rearrange("p (t d) -> p t d", t=BT),
                              ACT.Copy).then_inc(done, 1)

            for taken in counts_taken:
                ac.sem_inc(taken, B0)
            ac.sem_inc(sums_taken, 2)
            ac.wait_ge(deg_ready, 1)
            ac.activation(deg[:, 1, :], deg[:, 0, :], ACT.Sqrt).then_inc(root_ready, 1)

            def round_part(part):
                for h, tiles in enumerate((slice(0, NT // 2), slice(NT // 2, NT))):
                    ac.wait_ge(left_made, part * 2 + h + 1)
                    ac.activation(xs_part[:, part, tiles, 0:D], xs[:, tiles, :], ACT.Copy).then_inc(part_rounded, 1)

            round_part(0)
            for g in range(TB):
                ac.wait_ge(xw_made, g + 1)
                to_xw(g, (0, 4, 5, 6, 7)[g], xw_taken)
            round_part(1)

            ac.wait_ge(sweeps_ready, 1)
            n_sweeps = ac.value_load(sweeps_i[0:1, 0:1], min_val=1, max_val=SWEEPS0)

            def take_counts(sweep, b, parity, q):
                for g in range(NG):
                    ac.wait_ge(counts_made[g], sweep * NS + b * B0 + q + 1)
                    ac.activation(counts[parity][:, :, q * VC + g * W0:q * VC + (g + 1) * W0],
                                  bank[g][:, 0:KEYS].rearrange("p (a b) -> p a b", a=NT), ACT.Copy).then_inc(counts_taken[g], 1)

            def take_sums(sweep, b, parity, supers):
                ac.wait_ge(sums_made, sweep * (NB + 1) + b + 1)
                ac.wait_ge(window_added, sweep * (NS * NG) + b * (B0 * NG) + 1)
                ac.activation(window_sums[:, 0:supers * VC], bank[4 + parity][0:DE, 0:supers * VC],
                              ACT.Copy).then_inc(sums_taken, 1)

            def batch(sweep, b, parity):
                for q in range(B0):
                    take_counts(sweep, b, parity, q)

            with ac.Fori(0, n_sweeps) as sweep:
                batch(sweep, 0, 0)
                with ac.Fori(0, NB // 2) as k:
                    for b, parity in ((k * 2 + 1, 1), (k * 2 + 2, 0)):
                        batch(sweep, b, parity)
                        take_sums(sweep, b - 1, 1 - parity, B0)
                take_counts(sweep, NB, NB % 2, 0)
                take_sums(sweep, NB - 1, 1 - NB % 2, B0)
                take_sums(sweep, NB, NB % 2, NS - NB * B0)

            ac.wait_ge(deg_ready, 2)
            ac.activation(deg[:, 1, :], deg[:, 0, :], ACT.Sqrt).then_inc(root_ready, 1)
            ac.wait_ge(var_ready, 1)
            ac.activation(deg[:, 1, :], norms[:, 3, :], ACT.Sqrt).then_inc(std_ready, 1)

            def end_norm(target, nth, ready, store):
                ac.wait_ge(shift_ready, nth)
                for g in range(DVE_GROUPS, TB):
                    for t in range(g * BT, (g + 1) * BT):
                        made = ac.activation(target[:, t, :], xw[:, t, :], ACT.Identity, bias=norms[:, 4, t:t + 1],
                                             scale=deg[:, 2, t:t + 1])
                    made.then_inc(ready, 1)
                    store(g)

            def store_x1(g):
                ac.wait_ge(x1_ready_act, g + 1 - DVE_GROUPS)
                ac.dma_start(x1_rows(g), x1[:, g * BT:(g + 1) * BT, :]).then_inc(x1_stored, 16)

            end_norm(x1, 1, x1_ready_act, store_x1)
            ac.wait_ge(x1_ready, DVE_GROUPS)
            ac.wait_ge(x1_ready_act, TB - DVE_GROUPS)
            ac.activation(x1_part[:, 0, :, :], x1[:, :, :], ACT.Copy).then_inc(x1_rounded, 1)

            for k in range(-(-NT // 4)):
                tiles = min(4, NT - k * 4)
                ac.wait_ge(turned, k + 1)
                ac.activation(x1T[0:D, k * 4 * P:(k * 4 + tiles) * P], bank[k][0:D, 0:tiles * P], ACT.Copy).then_inc(turn_taken, 1)

            ac.wait_ge(x1_left_made, 1)
            ac.activation(x1_part[:, 1, :, :], x1_left[:, :, :], ACT.Copy).then_inc(x1_rounded, 1)

            for g in range(TB):
                ac.wait_ge(self_made, g + 1)
                to_xw(g, (7, 0, 1, 2, 3)[g], self_taken)

            n_sweeps = ac.value_load(sweeps_i[0:1, 1:2], min_val=1, max_val=SWEEPS1)
            ac.sem_inc(hidden_ready, 8)

            def rectify(sweep, i, slot):
                n = sweep * NS + i
                ac.wait_ge(weights_made, n * 2 + 2)
                for h in range(2):
                    ac.wait_ge(hidden_made, n * 2 + h + 1)
                    ac.activation(hidden[0:D, slot, h * 512:(h + 1) * 512], bank[h][0:D, :], ACT.Relu,
                                  bias=b1_sb[:, 0:1]).then_inc(hidden_ready, 1)

            def round_first(n, slot, nth, place):
                ac.wait_ge(attrs_in[slot], (nth + 1) * 16)
                ac.activation(ea_round[place], ea_sb[:, slot, :], ACT.Copy).then_inc(rounded, 1)

            def round_second(n, place):
                ac.wait_ge(left_ready, n + 5)
                ac.activation(ea_mid[place], ea_left[place], ACT.Copy).then_inc(mid_ready, 1)

            def rounds_of(sweep, i, ahead):
                return sweep * per_slot[(i + ahead) % SLOTS]

            with ac.Fori(0, n_sweeps) as sweep:
                ac.wait_ge(weights_made, sweep * (NS * 2) + 4)
                ac.sem_inc(carrier, 1)
                for i in range(2):
                    round_first(sweep * NS + i, i, rounds_of(sweep, i, 0), i)
                for i in range(2):
                    round_second(sweep * NS + i, i)
                round_first(sweep * NS + 2, 2, rounds_of(sweep, 2, 0), 0)
                rectify(sweep, 0, 0)
                with ac.Fori(0, rounds - 1) as k:
                    for slot in range(SLOTS):
                        i = k * SLOTS + slot
                        rectify(sweep, i + 1, (slot + 1) % 2)
                        round_second(sweep * NS + i + 2, slot % 2)
                        round_first(sweep * NS + i + 3, (slot + 3) % SLOTS,
                                    rounds_of(sweep, slot, 3) + k + (slot + 3) // SLOTS, (slot + 1) % 2)
                for i in range(NS - 1 - SLOTS, NS - 1):
                    rectify(sweep, i + 1, (i + 1) % 2)
                    if i + 2 < NS:
                        round_second(sweep * NS + i + 2, i % 2)
                    if i + 3 < NS:
                        round_first(sweep * NS + i + 3, (i + 3) % SLOTS, rounds_of(sweep, i, 3) + (i + 3) // SLOTS, (i + 1) % 2)
            ac.wait_ge(var_ready, 2)
            ac.activation(deg[:, 1, :], norms[:, 3, :], ACT.Sqrt).then_inc(std_ready, 1)

            def store_y(g):
                ac.wait_ge(y_ready_act, g + 1 - DVE_GROUPS)
                rows = min((g + 1) * BT, NODES // P) - g * BT
                ac.dma_start(out[g * BT * P:(g * BT + rows) * P, :].rearrange("(t p) d -> p t d", p=P),
                             y[:, g * BT:g * BT + rows, :]).then_inc(out_stored, 16)

            end_norm(y, 2, y_ready_act, store_y)

        @block.tensor
        def _(te):
            te.wait_ge(const_ready, CONSTS)

            te.sem_inc(hist_used, 2)
            tally = bank[1][0:LO, 0:HI]
            te.matmul(tally, zeros[:, 0:LO], zeros[:, 0:HI], start=True, stop=False)

            def hist(n, slot, chunks=HC):
                te.wait_ge(hist_ready, n + 1)
                for c in range(chunks):
                    made = te.matmul(tally, lo_hot[:, slot, c // IC, :, c % IC], hi_hot[:, slot, c // IC, :, c % IC],
                                     start=False, stop=False)
                made.then_inc(hist_used, 1)

            with te.Fori(0, HISTS // HIST_UNROLL) as k:
                for m in range(HIST_UNROLL):
                    hist(k * HIST_UNROLL + m, m % 2)
            for n in range(HISTS // HIST_UNROLL * HIST_UNROLL, HISTS):
                hist(n, n % 2)
            hist(HISTS, HISTS % 2, CH)
            te.matmul(tally, zeros[:, 0:LO], zeros[:, 0:HI], start=False, stop=True).then_inc(hist_done, 1)

            def project(first, last):
                for g in range(first, last):
                    for t in range(BT):
                        at = (g * BT + t) * P
                        made = te.matmul(bank[(0, 4, 5, 6, 7)[g]][:, t * D:(t + 1) * D], xT[:, at:at + P], w0_sb[0:D, 0:D],
                                         start=True, stop=True)
                    made.then_inc(xw_made, 1)

            te.wait_ge(weights_in, 8 * 16)
            project(0, 3)
            te.wait_ge(diag_ready, 1)
            for a, z in ((0, 4), (4, NG + 3)):
                made = te.matmul(bank[2 + a // 4][:, 0:(z - a) * NS], ones[0:NS, :], diag[:, a:z, :].rearrange("p a b -> p (a b)"),
                                 start=True, stop=True)
            made.then_inc(bases_spread, 1)
            project(3, TB)

            te.wait_ge(sweeps_ready, 1)
            n_sweeps = te.value_load(sweeps_i[0:1, 0:1], min_val=1, max_val=SWEEPS0)
            te.wait_ge(xw_taken, TB)

            def count(sweep, b, q):
                n = sweep * NS + b * B0 + q
                te.wait_ge(hots_ready, n + 1)
                for g in range(NG):
                    te.wait_ge(counts_taken[g], n + B0)
                    for c in range(g * GC, (g + 1) * GC):
                        made = te.matmul(bank[g][:, 0:KEYS], low_hot[:, q, c // IC, :, c % IC], key_hot[:, q, c // IC, :, c % IC],
                                         start=c == g * GC, stop=c == (g + 1) * GC - 1)
                    made.then_inc(counts_made[g], 1)

            def sums(sweep, b, parity, supers, quarter):
                if quarter == 0:
                    for g in range(NG):
                        te.wait_ge(counts_taken[g], sweep * NS + b * B0 + supers + B0)
                    te.wait_ge(sums_taken, sweep * (NB + 1) + b + 1)
                for a in range(quarter * NT // 4, (quarter + 1) * NT // 4):
                    for part in range(3):
                        made = te.matmul(bank[4 + parity][0:DE, 0:supers * VC], xs_part[:, part, a, :],
                                         counts[parity][:, a, 0:supers * VC],
                                         start=a == part == 0, stop=a == NT - 1 and part == 2)
                if quarter == 3:
                    made.then_inc(sums_made, 1)

            with te.Fori(0, n_sweeps) as sweep:
                for q in range(B0):
                    count(sweep, 0, q)
                te.wait_ge(xs_ready, 2)
                with te.Fori(0, NB // 2) as k:
                    for b, parity in ((k * 2 + 1, 1), (k * 2 + 2, 0)):
                        for q in range(B0):
                            count(sweep, b, q)
                            sums(sweep, b - 1, 1 - parity, B0, q)
                count(sweep, NB, 0)
                for quarter in range(4):
                    sums(sweep, NB - 1, 1 - NB % 2, B0, quarter)
                for quarter in range(4):
                    sums(sweep, NB, NB % 2, NS - NB * B0, quarter)

            te.wait_ge(layer0_done, 1)
            for g in range(TB):
                for t in range(BT):
                    at = (g * BT + t) * P
                    made = te.matmul(bank[1 + g][:, t * DE:(t + 1) * DE], agg0T[:, at:at + P], w0_sb[:, :], start=True, stop=True)
                made.then_inc(agg_made, 1)

            for k in range(-(-NT // 4)):
                tiles = min(4, NT - k * 4)
                last_group = (k * 4 + tiles - 1) // BT
                if last_group < DVE_GROUPS:
                    te.wait_ge(x1_ready, last_group + 1)
                else:
                    te.wait_ge(x1_ready, DVE_GROUPS)
                    te.wait_ge(x1_ready_act, last_group + 1 - DVE_GROUPS)
                for t in range(tiles):
                    made = te.transpose(bank[k][0:D, t * P:(t + 1) * P], x1[:, k * 4 + t, :], ident[:, :])
                made.then_inc(turned, 1)

            te.wait_ge(late_const, LATE)
            for g in range(TB):
                te.wait_ge(turn_taken, min(-(-NT // 4), (g + 1) * BT // 4 + 1))
                for t in range(BT):
                    at = (g * BT + t) * P
                    made = te.matmul(bank[(7, 0, 1, 2, 3)[g]][:, t * D:(t + 1) * D], x1T[:, at:at + P], ws_sb[:, :],
                                     start=True, stop=True)
                made.then_inc(self_made, 1)

            n_sweeps = te.value_load(sweeps_i[0:1, 1:2], min_val=1, max_val=SWEEPS1)
            te.sem_inc(weights_made, 4)
            te.sem_inc(window_made, 2)
            te.wait_ge(self_taken, TB)

            def hide(n, place, h):
                te.wait_ge(parts_ready, n + 2)
                te.wait_ge(hidden_ready, n * 2 + h + 7)
                te.matmul(bank[h][0:D, :], w1_sb[:, 0, :], ea_parts[place][:, h * 512:(h + 1) * 512], start=True, stop=False)
                te.matmul(bank[h][0:D, :], w1_sb[:, 1, :], ea_parts[place][:, h * 512:(h + 1) * 512], start=False,
                          stop=True).then_inc(hidden_made, 1)

            def weigh(n, slot, h):
                te.wait_ge(hidden_ready, n * 2 + h + 9)
                te.wait_ge(messages_ready, n * 2 + h + 5)
                for c in range(CH // 2):
                    at = h * 512 + c * P
                    made = te.matmul(bank[2 + 2 * (slot % 2) + h][:, c * D:(c + 1) * D], hidden[:, slot % 2, at:at + P],
                                     w2_sb[:, :], start=True, stop=True)
                if h == DENSE * 2 // CH:
                    te.wait_ge(node_hot_ready, n + 1)
                    for t in range(NT):
                        for part in range(3):
                            made = te.matmul(bank[2 + 2 * (slot % 2) + h][:, CH // 2 * D:(CH // 2 + 1) * D], node_hot[slot % 2][:, t, :],
                                             x1_part[:, part, t, :], start=t == part == 0, stop=t == NT - 1 and part == 2)
                made.then_inc(weights_made, 1)

            def gather_sums(n, slot, h):
                if h == 0:
                    te.wait_ge(hot_ready, n + 1)
                    te.wait_ge(window_taken, n + 1)
                te.wait_ge(messages_ready, n * 2 + h + 9)
                for c in range(h * CH // 2, (h + 1) * CH // 2):
                    made = te.matmul(bank[6 + slot % 2][0:D, 0:W1], messages[slot % 2][:, c, :], dst_hot[slot % 2][:, c, :],
                                     start=c == 0, stop=c == CH - 1)
                if h == 1:
                    made.then_inc(window_made, 1)

            with te.Fori(0, n_sweeps) as sweep:
                te.wait_ge(messages_ready, sweep * (NS * 2) + 8)
                te.wait_ge(window_taken, sweep * NS + 2)
                te.sem_inc(carrier, 1)
                for h in range(2):
                    hide(sweep * NS, 0, h)
                for h in range(2):
                    weigh(sweep * NS, 0, h)
                with te.Fori(0, rounds) as k:
                    for slot in range(SLOTS):
                        n = sweep * NS + k * SLOTS + slot
                        after = (slot + 1) % SLOTS
                        for h in range(2):
                            hide(n + 1, after % 2, h)
                        for h in range(2):
                            gather_sums(n, slot, h)
                            weigh(n + 1, after, h)
                for h in range(2):
                    gather_sums(sweep * NS + NS - 1, 0, h)

            te.wait_ge(layer1_done, 1)
            for g in range(TB):
                for t in range(BT):
                    at = (g * BT + t) * P
                    made = te.matmul(bank[g][:, t * D:(t + 1) * D], agg1T[:, at:at + P], wn_sb[:, :], start=True, stop=True)
                made.then_inc(sums1_made, 1)


def kernel(x, src, dst, edge_attr_17, L0_gnn_weight, L0_gnn_bias, L1_gnn_W1, L1_gnn_b1, L1_gnn_W2, L1_gnn_b2,
           L1_gnn_Ws, L1_gnn_bs, L1_gnn_Wn, L1_gnn_bn):
    import numpy as np
    import concourse.bacc as bacc
    from concourse.bass_utils import run_bass_kernel_spmd

    def padded(a, shape, fill=0):
        a = np.asarray(a)
        whole = np.full(shape, fill, a.dtype)
        whole[tuple(slice(0, n) for n in a.shape)] = a
        return whole

    x = np.asarray(x)
    src_pad, dst_pad = padded(src, (NC * P,), PAD_SRC), padded(dst, (NC * P,), PAD_DST)
    weight = padded(L0_gnn_weight, (DE, DE))
    weight[D, D] = 1
    x_pad = padded(x, (NP, D))

    def with_bias(w, b):
        return np.concatenate([np.asarray(w).T, np.asarray(b)[None]])

    rows = np.repeat(np.arange(len(ROW_PARTS)), ED)
    part_masks = np.stack([-1.0 * (np.array(ROW_PARTS)[rows] > n) for n in (1, 2)]
                          + [np.array(parts)[rows] == n for parts in W_PARTS for n in (1, 2, 3)], 1).astype(np.float32)

    arrays = {
        "x_rows": x_pad,
        "x_cols": x_pad.T,
        "src_pm": src_pad.reshape(NC, P).T,
        "src_rows": src_pad.reshape(NS, SG),
        "dst_pm": dst_pad.reshape(NC, P).T,
        "dst_rows": dst_pad.reshape(NS, SG),
        "ea_cols": np.tile(padded(edge_attr_17, (NC * P, ED)).T, (len(ROW_PARTS), 1)),
        "w0e": weight,
        "b0": np.asarray(L0_gnn_bias)[None],
        "w1t": np.tile(np.asarray(L1_gnn_W1).T, (len(ROW_PARTS), 1)),
        "b1c": np.asarray(L1_gnn_b1)[:, None],
        "w2e": with_bias(L1_gnn_W2, L1_gnn_b2),
        "wse": np.concatenate([with_bias(L1_gnn_Ws, L1_gnn_bs), np.asarray(L1_gnn_bn)[None]]),
        "wnt": np.asarray(L1_gnn_Wn).T,
        "part_masks": part_masks,
    }
    arrays = {name: np.ascontiguousarray(a) for name, a in arrays.items()}
    nc = bacc.Bacc("TRN2", target_bir_lowering=False, num_devices=1)
    args = [nc.dram_tensor(name, a.shape, mybir.dt.from_np(a.dtype), kind="ExternalInput").ap() for name, a in arrays.items()]
    out = nc.dram_tensor("out", (NODES, D), mybir.dt.float32, kind="ExternalOutput").ap()
    build(nc, *args, out)
    return run_bass_kernel_spmd(nc, [arrays], core_ids=[0]).results[0]["out"]
```
